# Optimizing a Trainium2 kernel written in Bass

```python
import numpy as np
import jax
import jax.numpy as jnp

def _softmax(x, axis=-1):
    return jax.nn.softmax(x, axis=axis)

def _gelu(x):
    return jax.nn.gelu(x, approximate=True)

def _silu(x):
    return jax.nn.silu(x)

def _sigmoid(x):
    return jax.nn.sigmoid(x)

def _layernorm(x, axis=-1, eps=1e-05):
    m = jnp.mean(x, axis=axis, keepdims=True)
    v = jnp.var(x, axis=axis, keepdims=True)
    return (x - m) / jnp.sqrt(v + eps)

def _scatter_add(tgt, idx, src, axis=0):
    return tgt.at[idx].add(src)

def _segment_sum(src, seg, n):
    return jax.ops.segment_sum(src, seg, n)
kernel_name = 'mk_xattn_seq_d2_seqx_r8_9d7c83'

def setup_inputs(seed: int=0):
    np.random.seed(seed)
    _w = jnp.asarray

    def _rec_inputs():
        import jax
        import jax.numpy as jnp
        _rk = jax.random.key(seed)
        x = 7.22e-05 + 1 * jax.random.normal(jax.random.fold_in(_rk, 1), (32, 64, 128), jnp.float32)
        _lenS = 64 - jax.random.randint(jax.random.fold_in(_rk, 7), (32,), 0, max(1, 64 // 4) + 1, jnp.int32)
        _lenS2 = 64 - jax.random.randint(jax.random.fold_in(_rk, 8), (32,), 0, max(1, 64 // 4) + 1, jnp.int32)
        _ctx_768P = jax.random.normal(jax.random.fold_in(_rk, 11), (32, 16, 96), jnp.float32)
        _ctx_768c = jax.random.dirichlet(jax.random.fold_in(_rk, 511), 0.3 * jnp.ones((16,), jnp.float32), (32, 64))
        _ctx_768t = jnp.einsum('bsk,bkd->bsd', _ctx_768c, _ctx_768P)
        _ctx_768t = _ctx_768t * jax.lax.rsqrt(jnp.mean(jnp.square(_ctx_768t)) + 1e-12) * 0.953939
        ctx_768 = 0.000651243 + 0.998673 * (_ctx_768t + 0.3 * jax.random.normal(jax.random.fold_in(_rk, 611), (32, 64, 96), jnp.float32))
        return (x, ctx_768)
    x, ctx_768 = _rec_inputs()

    def _L0_xattn_setup():
        import jax, jax.numpy as jnp
        import numpy as np
        HEADS = 16
        D_HEAD = 64
        EPS = 1e-05

        def _ln(x, g, b):
            m = jnp.mean(x, axis=-1, keepdims=True)
            v = jnp.var(x, axis=-1, keepdims=True)
            return (x - m) * jax.lax.rsqrt(v + EPS) * g + b

        def _attn(xq, xc, Wq, Wk, Wv, Wo, bo):
            B, N, _ = xq.shape
            S = xc.shape[1]
            q = (xq @ Wq).reshape(B, N, HEADS, D_HEAD)
            k = (xc @ Wk).reshape(B, S, HEADS, D_HEAD)
            v = (xc @ Wv).reshape(B, S, HEADS, D_HEAD)
            scale = D_HEAD ** (-0.5)
            scores = jnp.einsum('bnhd,bshd->bhns', q, k) * scale
            attn = jax.nn.softmax(scores, axis=-1)
            out = jnp.einsum('bhns,bshd->bnhd', attn, v).reshape(B, N, HEADS * D_HEAD)
            return out @ Wo + bo

        def _geglu_ff(x, Wp, bp, Wf, bf):
            h = x @ Wp + bp
            a, gate = jnp.split(h, 2, axis=-1)
            return a * jax.nn.gelu(gate, approximate=False) @ Wf + bf
        key = jax.random.key(seed)
        ks = jax.random.split(key, 16)
        dim, ctx, inner, ffin = (128, 96, HEADS * D_HEAD, 4 * 128)

        def w(k, i, o):
            return jax.random.normal(k, (i, o), jnp.float32) * i ** (-0.5)
        inp = {'x': jax.random.normal(ks[0], (4, 256, dim), jnp.float32), 'context': jax.random.normal(ks[1], (4, 77, ctx), jnp.float32), 'Wq1': w(ks[2], dim, inner), 'Wk1': w(ks[3], dim, inner), 'Wv1': w(ks[4], dim, inner), 'Wo1': w(ks[5], inner, dim), 'bo1': jnp.zeros((dim,), jnp.float32), 'Wq2': w(ks[6], dim, inner), 'Wk2': w(ks[7], ctx, inner), 'Wv2': w(ks[8], ctx, inner), 'Wo2': w(ks[9], inner, dim), 'bo2': jnp.zeros((dim,), jnp.float32), 'Wp': w(ks[10], dim, 2 * ffin), 'bp': jnp.zeros((2 * ffin,), jnp.float32), 'Wf': w(ks[11], ffin, dim), 'bf': jnp.zeros((dim,), jnp.float32), 'g1': jnp.ones((dim,), jnp.float32), 'b1': jnp.zeros((dim,), jnp.float32), 'g2': jnp.ones((dim,), jnp.float32), 'b2': jnp.zeros((dim,), jnp.float32), 'g3': jnp.ones((dim,), jnp.float32), 'b3': jnp.zeros((dim,), jnp.float32)}
        return inp
    _L0_xattn_all = _L0_xattn_setup()
    _L0_xattn_in = {k: v for k, v in _L0_xattn_all.items() if k in ('Wq1', 'Wk1', 'Wv1', 'Wo1', 'bo1', 'Wq2', 'Wk2', 'Wv2', 'Wo2', 'bo2', 'Wp', 'bp', 'Wf', 'bf', 'g1', 'b1', 'g2', 'b2', 'g3', 'b3')}
    del _L0_xattn_all

    def _L1_xattn_setup():
        import jax, jax.numpy as jnp
        import numpy as np
        LATENT = 128
        TEXT = 96
        HEADS = 16
        HEAD_DIM = LATENT // HEADS
        SCALE = HEAD_DIM ** (-0.5)
        LN_EPS = 1e-05
        key = jax.random.key(seed)
        ks = jax.random.split(key, 16)
        B, Tx, Txf = (4, 512, 32)

        def lin(k, fan_in, fan_out):
            bound = 1.0 / np.sqrt(fan_in)
            kw, kb = jax.random.split(k)
            W = jax.random.uniform(kw, (fan_in, fan_out), jnp.float32, -bound, bound)
            b = jax.random.uniform(kb, (fan_out,), jnp.float32, -bound, bound)
            return (W, b)
        Wq, bq = lin(ks[0], LATENT, LATENT)
        Wk, bk = lin(ks[1], TEXT, LATENT)
        Wv, bv = lin(ks[2], TEXT, LATENT)
        Wo, bo = lin(ks[3], LATENT, LATENT)
        W1, b1 = lin(ks[4], LATENT, 4 * LATENT)
        W2, b2 = lin(ks[5], 4 * LATENT, LATENT)
        return {'x': jax.random.normal(ks[6], (B, Tx, LATENT), jnp.float32), 'xf': jax.random.normal(ks[7], (B, Txf, TEXT), jnp.float32), 'Wq': Wq, 'bq': bq, 'Wk': Wk, 'bk': bk, 'Wv': Wv, 'bv': bv, 'Wo': Wo, 'bo': bo, 'ln_g': jnp.ones((LATENT,), jnp.float32), 'ln_b': jnp.zeros((LATENT,), jnp.float32), 'W1': W1, 'b1': b1, 'W2': W2, 'b2': b2}
    _L1_xattn_all = _L1_xattn_setup()
    _L1_xattn_in = {k: v for k, v in _L1_xattn_all.items() if k in ('Wq', 'bq', 'Wk', 'bk', 'Wv', 'bv', 'Wo', 'bo', 'ln_g', 'ln_b', 'W1', 'b1', 'W2', 'b2')}
    del _L1_xattn_all
    return {'x': x, 'ctx_768': ctx_768, 'L0_xattn_Wq1': _L0_xattn_in['Wq1'], 'L0_xattn_Wk1': _L0_xattn_in['Wk1'], 'L0_xattn_Wv1': _L0_xattn_in['Wv1'], 'L0_xattn_Wo1': _L0_xattn_in['Wo1'], 'L0_xattn_bo1': _L0_xattn_in['bo1'], 'L0_xattn_Wq2': _L0_xattn_in['Wq2'], 'L0_xattn_Wk2': _L0_xattn_in['Wk2'], 'L0_xattn_Wv2': _L0_xattn_in['Wv2'], 'L0_xattn_Wo2': _L0_xattn_in['Wo2'], 'L0_xattn_bo2': _L0_xattn_in['bo2'], 'L0_xattn_Wp': _L0_xattn_in['Wp'], 'L0_xattn_bp': _L0_xattn_in['bp'], 'L0_xattn_Wf': _L0_xattn_in['Wf'], 'L0_xattn_bf': _L0_xattn_in['bf'], 'L0_xattn_g1': _L0_xattn_in['g1'], 'L0_xattn_b1': _L0_xattn_in['b1'], 'L0_xattn_g2': _L0_xattn_in['g2'], 'L0_xattn_b2': _L0_xattn_in['b2'], 'L0_xattn_g3': _L0_xattn_in['g3'], 'L0_xattn_b3': _L0_xattn_in['b3'], 'L1_xattn_Wq': _L1_xattn_in['Wq'], 'L1_xattn_bq': _L1_xattn_in['bq'], 'L1_xattn_Wk': _L1_xattn_in['Wk'], 'L1_xattn_bk': _L1_xattn_in['bk'], 'L1_xattn_Wv': _L1_xattn_in['Wv'], 'L1_xattn_bv': _L1_xattn_in['bv'], 'L1_xattn_Wo': _L1_xattn_in['Wo'], 'L1_xattn_bo': _L1_xattn_in['bo'], 'L1_xattn_ln_g': _L1_xattn_in['ln_g'], 'L1_xattn_ln_b': _L1_xattn_in['ln_b'], 'L1_xattn_W1': _L1_xattn_in['W1'], 'L1_xattn_b1': _L1_xattn_in['b1'], 'L1_xattn_W2': _L1_xattn_in['W2'], 'L1_xattn_b2': _L1_xattn_in['b2']}

def reference(x, ctx_768, L0_xattn_Wq1, L0_xattn_Wk1, L0_xattn_Wv1, L0_xattn_Wo1, L0_xattn_bo1, L0_xattn_Wq2, L0_xattn_Wk2, L0_xattn_Wv2, L0_xattn_Wo2, L0_xattn_bo2, L0_xattn_Wp, L0_xattn_bp, L0_xattn_Wf, L0_xattn_bf, L0_xattn_g1, L0_xattn_b1, L0_xattn_g2, L0_xattn_b2, L0_xattn_g3, L0_xattn_b3, L1_xattn_Wq, L1_xattn_bq, L1_xattn_Wk, L1_xattn_bk, L1_xattn_Wv, L1_xattn_bv, L1_xattn_Wo, L1_xattn_bo, L1_xattn_ln_g, L1_xattn_ln_b, L1_xattn_W1, L1_xattn_b1, L1_xattn_W2, L1_xattn_b2):
    import jax
    import jax.numpy as jnp

    def _L0_xattn_ref(x, context, Wq1, Wk1, Wv1, Wo1, bo1, Wq2, Wk2, Wv2, Wo2, bo2, Wp, bp, Wf, bf, g1, b1, g2, b2, g3, b3):
        import jax, jax.numpy as jnp
        import numpy as np
        HEADS = 16
        D_HEAD = 64
        EPS = 1e-05

        def _ln(x, g, b):
            m = jnp.mean(x, axis=-1, keepdims=True)
            v = jnp.var(x, axis=-1, keepdims=True)
            return (x - m) * jax.lax.rsqrt(v + EPS) * g + b

        def _attn(xq, xc, Wq, Wk, Wv, Wo, bo):
            B, N, _ = xq.shape
            S = xc.shape[1]
            q = (xq @ Wq).reshape(B, N, HEADS, D_HEAD)
            k = (xc @ Wk).reshape(B, S, HEADS, D_HEAD)
            v = (xc @ Wv).reshape(B, S, HEADS, D_HEAD)
            scale = D_HEAD ** (-0.5)
            scores = jnp.einsum('bnhd,bshd->bhns', q, k) * scale
            attn = jax.nn.softmax(scores, axis=-1)
            out = jnp.einsum('bhns,bshd->bnhd', attn, v).reshape(B, N, HEADS * D_HEAD)
            return out @ Wo + bo

        def _geglu_ff(x, Wp, bp, Wf, bf):
            h = x @ Wp + bp
            a, gate = jnp.split(h, 2, axis=-1)
            return a * jax.nn.gelu(gate, approximate=False) @ Wf + bf
        x = _attn(_ln(x, g1, b1), _ln(x, g1, b1), Wq1, Wk1, Wv1, Wo1, bo1) + x
        x = _attn(_ln(x, g2, b2), context, Wq2, Wk2, Wv2, Wo2, bo2) + x
        x = _geglu_ff(_ln(x, g3, b3), Wp, bp, Wf, bf) + x
        return x

    def _L1_xattn_ref(x, xf, Wq, bq, Wk, bk, Wv, bv, Wo, bo, ln_g, ln_b, W1, b1, W2, b2):
        import jax, jax.numpy as jnp
        import numpy as np
        LATENT = 128
        TEXT = 96
        HEADS = 16
        HEAD_DIM = LATENT // HEADS
        SCALE = HEAD_DIM ** (-0.5)
        LN_EPS = 1e-05
        B, Tx, D = x.shape
        Txf = xf.shape[1]
        q = (x @ Wq + bq).reshape(B, Tx, HEADS, HEAD_DIM).transpose(0, 2, 1, 3)
        k = (xf @ Wk + bk).reshape(B, Txf, HEADS, HEAD_DIM).transpose(0, 2, 1, 3)
        v = (xf @ Wv + bv).reshape(B, Txf, HEADS, HEAD_DIM).transpose(0, 2, 1, 3)
        scores = jnp.einsum('bhqd,bhkd->bhqk', q * SCALE, k)
        probs = jax.nn.softmax(scores, axis=-1)
        attn = jnp.einsum('bhqk,bhkd->bhqd', probs, v)
        out = attn.transpose(0, 2, 1, 3).reshape(B, Tx, D)
        out = out @ Wo + bo
        mu = jnp.mean(out, axis=-1, keepdims=True)
        var = jnp.var(out, axis=-1, keepdims=True)
        h = (out - mu) * jax.lax.rsqrt(var + LN_EPS) * ln_g + ln_b
        h = jax.nn.gelu(h @ W1 + b1, approximate=False)
        ffn = h @ W2 + b2
        out = out + ffn
        return x + out
    x = _L0_xattn_ref(x, ctx_768, L0_xattn_Wq1, L0_xattn_Wk1, L0_xattn_Wv1, L0_xattn_Wo1, L0_xattn_bo1, L0_xattn_Wq2, L0_xattn_Wk2, L0_xattn_Wv2, L0_xattn_Wo2, L0_xattn_bo2, L0_xattn_Wp, L0_xattn_bp, L0_xattn_Wf, L0_xattn_bf, L0_xattn_g1, L0_xattn_b1, L0_xattn_g2, L0_xattn_b2, L0_xattn_g3, L0_xattn_b3)
    x = _L1_xattn_ref(x, ctx_768, L1_xattn_Wq, L1_xattn_bq, L1_xattn_Wk, L1_xattn_bk, L1_xattn_Wv, L1_xattn_bv, L1_xattn_Wo, L1_xattn_bo, L1_xattn_ln_g, L1_xattn_ln_b, L1_xattn_W1, L1_xattn_b1, L1_xattn_W2, L1_xattn_b2)
    return x

_drawn_inputs = setup_inputs


def setup_inputs(seed=0):
    import zlib

    import numpy as np

    out = dict(_drawn_inputs(seed))
    spreads = {'L0_xattn_bo1': (0.0, 0.1),
     'L0_xattn_bo2': (0.0, 0.1),
     'L0_xattn_bp': (0.0, 0.1),
     'L0_xattn_bf': (0.0, 0.1),
     'L0_xattn_g1': (1.0, 0.2),
     'L0_xattn_b1': (0.0, 0.1),
     'L0_xattn_g2': (1.0, 0.2),
     'L0_xattn_b2': (0.0, 0.364),
     'L0_xattn_g3': (1.0, 0.2),
     'L0_xattn_b3': (0.0, 0.1),
     'L1_xattn_ln_g': (1.0, 0.2),
     'L1_xattn_ln_b': (0.0, 0.5)}
    factors = {'L1_xattn_bq': 26.188, 'L1_xattn_bk': 64.0, 'L1_xattn_b1': 4.459, 'L1_xattn_b2': 3.097}
    for name, (base, spread) in spreads.items():
        noise = np.random.default_rng([zlib.crc32(name.encode()), seed]).standard_normal(out[name].shape)
        drawn = base * np.exp(spread * noise) if base else spread * noise
        out[name] = jnp.asarray(drawn.astype(out[name].dtype))
    for name, factor in factors.items():
        out[name] = (out[name] * factor).astype(out[name].dtype)
    return out
```

```python
import concourse.bass as bass
from concourse import mybir
from contextlib import ExitStack

F32 = mybir.dt.float32
F32R = mybir.dt.float32r
ACT = mybir.ActivationFunctionType
ALU = mybir.AluOpType
AX = mybir.AxisListType

B, N, D, C = 32, 64, 128, 96
H, DH = 16, 64
H1 = D // H
FF = 4 * D
EPS = 1e-5
ROWS = 128
TILES = B * N // ROWS
T = 2
GB = T * ROWS // N
GR = T * ROWS
GROUPS = TILES // T
PAIRS = H // 2
BANK = 512
SELF, CROSS, GEGLU, CROSS2, FFN = range(5)
PHASES = 5
WITH_CTX = (CROSS, CROSS2)

K_BY_DVE = (3, 4, 7)
Z_BY_ACT = (1, 4, 6)


def copiers(kind, i):
    if kind in ("fa", "fb"):
        return 1, 1
    if kind == "wt":
        return (1, 0) if i % 2 == 0 else (0, 1)
    if kind == "k":
        return (0, 1) if i in K_BY_DVE else (1, 0)
    if kind == "z":
        return (2, 0) if i in Z_BY_ACT else (1, 1)
    if kind in ("qk", "at", "up1"):
        return 1, 0
    return 0, 1


class Step:

    def __init__(self, phase, first, turn=None):
        self.phase, self.first, self.turn = phase, first, turn
        self.parity = first % 2

    def ahead(self, k):
        if self.first + k < GROUPS:
            return Step(self.phase, self.first + k, self.turn)
        assert self.turn is None
        return Step(self.phase + 1, self.first + k - GROUPS) if self.phase + 1 < PHASES else None

    def at(self, scale, offset=0):
        if self.turn is None:
            return self.first * scale + offset
        return self.turn * (2 * scale) + (self.first * scale + offset)


class Counts:

    def __init__(self):
        self.total, self.value, self.uses, self.start = {}, {}, [], {}
        for p in (SELF, CROSS):
            self.fold(p)
        self.x(SELF, 0)
        self.p(SELF, 0)
        self.x(SELF, 1)
        for p in range(PHASES):
            for g in range(GROUPS):
                self.group(p, g)

    def tick(self, name, key, n=1):
        self.total[name] = self.total.get(name, 0) + n
        self.value[(name, *key)] = self.total[name]

    def use(self, kind, p, g, i=0):
        self.tick("full", (kind, p, g, i))
        for name, n in zip(("act", "dve"), copiers("up1" if kind == "up" and p == FFN else kind, i)):
            self.tick(name, (kind, p, g, i), n)
        self.uses.append((kind, p, g, i))

    def fold(self, p):
        for kind, n in (("wt", 6), ("fa", 4), ("fb", 4)):
            for i in range(n):
                self.use(kind, p, 0, i)

    def x(self, p, g):
        if p != CROSS2:
            for name in ("stats", "mean", "eps", "rstd", "biased"):
                self.tick(name, (p, g))
        self.tick("normed", (p, g))
        if p != CROSS2:
            self.tick("high", (p, g))
            self.tick("rest", (p, g))
        if p in WITH_CTX:
            self.tick(f"ctx{g % 2}", (p, g), 16)
            self.tick("ctx_turned", (p, g))
        self.use("x", p, g)

    def p(self, p, g):
        for kind, n in {SELF: [("k", 8)], CROSS: [("k", 8)], CROSS2: [("qk", 1), ("v", 1)]}.get(p, [("up", 4)]):
            for i in range(n):
                self.use(kind, p, g, i)
                if kind == "up" and p == GEGLU:
                    self.tick("gelu", (p, g, i))
        if p == CROSS2:
            self.tick("masked", (p, g))

    def group(self, p, g):
        self.start[("act", p, g)] = self.total["act"]
        self.start[("dve", p, g)] = self.total["dve"]
        self.start[("uses", p, g)] = len(self.uses)
        one, two = Step(p, g).ahead(1), Step(p, g).ahead(2)
        if p in (SELF, CROSS, CROSS2):
            for t in range(T):
                for name in ("scores", "max", "shifted", "exp"):
                    self.tick(name, (p, g, t))
                if p != CROSS2:
                    for name in ("sums", "recip", "probs"):
                        self.tick(name, (p, g, t))
            if one:
                self.p(one.phase, one.first)
            if p != CROSS2:
                for i in range(8):
                    self.use("z", p, g, i)
            for t in range(T):
                for c in range(2):
                    self.tick("turned", (p, g, t, c))
                self.tick("pt_act", (p, g, t))
                self.tick("pt_dve", (p, g, t))
            if two:
                self.x(two.phase, two.first)
            self.tick("out0", (p, g))
            self.use("out1", p, g)
            if p == CROSS2:
                for t in range(T):
                    self.tick("norm", (p, g, t))
                self.use("at", p, g)
                self.use("wo", p, g)
        else:
            if one:
                self.p(one.phase, one.first)
            if two:
                self.x(two.phase, two.first)
            self.use("down", p, g)

    def linear(self, of, step):
        v = of(step.first)
        if step.turn is None:
            return v
        per = of(step.first + 2) - v
        assert of(step.first + 4) - of(step.first + 2) == per, step
        return step.turn * per + v

    def at(self, name, step, *rest, kind=None):
        head = (name,) if kind is None else (name, kind)
        tail = rest if kind is None else (rest or (0,))
        return self.linear(lambda g: self.value[(*head, step.phase, g, *tail)], step)

    def start_of(self, name, step):
        return self.linear(lambda g: self.start[(name, step.phase, g)], step)

    def bank(self, kind, step, i=0):
        return self.uses.index((kind, step.phase, step.first, i)) % 3


def attention_blocks(nc, w, out):
    cnt = Counts()
    ctx = ExitStack()
    with ctx:
        def sb(name, shape, dt=F32):
            return ctx.enter_context(nc.sbuf_tensor(name, shape, dt))

        def ps(name, shape):
            return ctx.enter_context(nc.psum_tensor(name, shape, F32))

        def sem(name):
            return ctx.enter_context(nc.semaphore(name))

        rows = sb("rows", [ROWS, TILES * D])
        rows2 = sb("rows2", [ROWS, TILES * D])
        ident = sb("ident", [128, 128])
        headmask = sb("headmask", [128, H])
        fold_a = [[sb(f"fold_a{p}{n}", [128, H, D], F32R) for n in "hr"] for p in (SELF, CROSS)]
        fold_b = [[sb(f"fold_b{p}{n}", [128, 2, PAIRS, D], F32R) for n in "hr"] for p in (SELF, CROSS)]
        wp = sb("wp", [D, 2 * FF])
        wp_s = [sb(f"wp_{n}", [D, 2 * FF], F32R) for n in "hr"]
        w1 = sb("w1", [D, FF])
        w1_s = [sb(f"w1_{n}", [D, FF], F32R) for n in "hr"]
        wf = sb("wf", [128, FF // 128, D])
        w2 = sb("w2", [128, FF // 128, D])
        wq1, wo1 = sb("wq1", [D, D]), sb("wo1", [D, D])
        wk1, wv1 = sb("wk1", [C, D]), sb("wv1", [C, D])
        cols = sb("cols", [128, 22])
        bias = sb("bias", [128, 6, D])
        neghalf = sb("neghalf", [128, T])
        eps = sb("eps", [128, T])
        seen = sb("seen", [ROWS, 1])
        ctx_in = [sb(f"ctx_in{n}", [ROWS, T, C]) for n in range(2)]
        stats = [sb(f"stats{n}", [128, T, 6]) for n in range(2)]
        mv = [sb(f"mv{n}", [128, T, 2]) for n in range(2)]
        veps = sb("veps", [128, T])
        rstd = [sb(f"rstd{n}", [128, T]) for n in range(2)]
        xn = sb("xn", [ROWS, T, D])
        xT = [sb(f"xT{n}", [D, GR]) for n in range(2)]
        cT = [sb(f"cT{n}", [C, GR]) for n in range(2)]
        src = [[sb(f"src{n}{m}", [D, GR], F32R) for m in "hr"] for n in range(2)]
        kt = sb("kt", [D, GB, H, N])
        zt = sb("zt", [128, GB, PAIRS, D])
        raw = {k: zt[:, n, :, :].rearrange("p a d -> p (a d)") for n, k in enumerate("kqvo")}
        turned_w = {k: kt[:, n, :, :].rearrange("p h n -> p (h n)").rearrange("p (a k) -> p a k", k=128)
                    for n, k in enumerate("kqv")}
        pr = [sb(f"pr{t}", [ROWS, H * N]) for t in range(T)]
        mx = sb("mx", [ROWS, T, H])
        sm = sb("sm", [ROWS, T, H])
        rc = sb("rc", [ROWS, T, H])
        pt = [sb(f"pt{t}", [128, PAIRS, ROWS]) for t in range(T)]
        ge = [sb(f"ge{n}", [128, GR]) for n in range(2)]
        hid = [sb(f"hid{n}", [128, FF // 128, GR]) for n in range(2)]
        qT, kT = sb("qT", [D, GR]), sb("kT", [D, GR])
        vb = [sb(f"vb{n}", [128, GB, PAIRS, 2 * (H1 + 1)]) for n in range(2)]
        att = sb("att", [ROWS, T, D])
        attT = sb("attT", [D, GR])

        G1, B1_, G2, B2_, G3, B3_, G4, B4_ = range(8)
        BQ, BK, BP, BF1 = 8, 9, 10, 18
        BO1, BO2, BFF, BO3, BV, BLAST = range(6)

        scp = ps("scp", [128, 4, BANK])
        stage = [ps(f"stage{n}", [128, BANK]) for n in range(3)]
        out0p = ps("out0p", [128, BANK])

        full = sem("stage_full")
        act = sem("stage_copied_act")
        dve = sem("stage_copied_dve")
        scores = sem("scores")
        maxed = sem("maxed")
        shifted = sem("shifted")
        exped = sem("exped")
        summed = sem("summed")
        recip = sem("recip")
        probs = sem("probs")
        turned = sem("turned")
        pt_act = sem("pt_act")
        pt_dve = sem("pt_dve")
        out0 = sem("out0")
        stated = sem("stated")
        meaned = sem("meaned")
        epsed = sem("epsed")
        rooted = sem("rooted")
        normed = sem("normed")
        biased = sem("biased")
        summed2 = sem("summed2")
        high = sem("high")
        rest = sem("rest")
        ctx_loaded = [sem("ctx_loaded0"), sem("ctx_loaded1")]
        ctx_turned = sem("ctx_turned")
        gelued = sem("gelued")
        masked = sem("masked")
        normr = sem("normr")
        loaded_rows = sem("loaded_rows")
        loaded_w = [sem("loaded_w0"), sem("loaded_w1")]
        loaded_small = sem("loaded_small")
        loaded_ffn = sem("loaded_ffn")
        made_ident = sem("made_ident")
        made_mask = sem("made_mask")
        made_half = sem("made_half")
        made_vb = sem("made_vb")
        raw_free = sem("raw_free")
        high_w = sem("high_w")
        rest_w = sem("rest_w")
        stored = sem("stored")

        scale = {SELF: DH ** -0.5, CROSS: DH ** -0.5, CROSS2: H1 ** -0.5}
        kdim = {SELF: D, CROSS: C}

        def row_slice(buf, step, t=0, n=1):
            return buf[:, bass.ds(step.at(T * D, t * D), n * D)]

        def each_group(eng, body):
            for p in range(PHASES):
                with eng.Fori(0, GROUPS // 2 - 1) as turn:
                    body(Step(p, 0, turn))
                    body(Step(p, 1, turn))
                body(Step(p, GROUPS - 2))
                body(Step(p, GROUPS - 1))

        def halves(ap):
            return ap.rearrange("p (h n) -> p h n", n=N)

        def loads_of(p):
            for key, name in zip("kqv", ("Wk", "Wq", "Wv")):
                k = C if p == CROSS and key != "q" else D
                yield raw[key][0:k, :], w[f"L0_xattn_{name}{p + 1}"]
            yield raw["o"].rearrange("p (a d) -> p a d", d=D), \
                w[f"L0_xattn_Wo{p + 1}"].rearrange("(a p) d -> p a d", p=128)

        def parts(kind, buf, c, e, k):
            if kind == "fa":
                return buf[0:k, 8 * c:8 * c + 8, :].rearrange("p (q e) d -> p q e d", e=2)[:, :, e, :]
            return buf[0:k, e, 4 * c:4 * c + 4, :]

        def key_copy(s, i):
            bank = stage[cnt.bank("k", s, i)]
            return (kt[:, :, 2 * i:2 * i + 2, :].rearrange("p b h n -> p h b n"),
                    bank[:, :].rearrange("p (h b n) -> p h b n", h=2, b=GB))

        def value_copy(s, i, b):
            t, e, c = i // 4, i // 2 % 2, i % 2
            bank = stage[cnt.bank("z", s, i)]
            return (zt[64 * e:64 * e + 64, 2 * t + b, 4 * c:4 * c + 4, :],
                    bank[64 * b:64 * b + 64, :].rearrange("p (a d) -> p a d", a=4))

        block = ctx.enter_context(nc.Block())

        @block.sync
        def _(sp):
            for dst, s in loads_of(SELF):
                sp.dma_start(dst, s).then_inc(loaded_w[0], 16)
            x = w["x"].rearrange("b n d -> (b n) d").rearrange("(t p) d -> p t d", p=ROWS)
            for q in range(4):
                n = TILES // 4
                sp.dma_start(rows[:, q * n * D:(q + 1) * n * D].rearrange("p (t d) -> p t d", d=D),
                             x[:, q * n:(q + 1) * n, :]).then_inc(loaded_rows, 16)
            sp.wait_ge(full, cnt.value[("full", "fb", SELF, 0, 3)])
            for dst, s in loads_of(CROSS):
                sp.dma_start(dst, s).then_inc(loaded_w[1], 16)
            for dst, s in ((wp[:, :], w["L0_xattn_Wp"]), (w1[:, :], w["L1_xattn_W1"]),
                           (wf[:, :, :], w["L0_xattn_Wf"].rearrange("(a p) d -> p a d", p=128)),
                           (w2[:, :, :], w["L1_xattn_W2"].rearrange("(a p) d -> p a d", p=128)),
                           (wq1[:, :], w["L1_xattn_Wq"]), (wk1[:, :], w["L1_xattn_Wk"]),
                           (wv1[:, :], w["L1_xattn_Wv"]), (wo1[:, :], w["L1_xattn_Wo"])):
                sp.dma_start(dst, s).then_inc(loaded_ffn, 16)
            c = w["ctx_768"].rearrange("b n d -> (b n) d").rearrange("(t p) d -> p t d", p=ROWS)

            def load_ctx(step):
                sp.dma_start(ctx_in[step.parity][:, :, :],
                             c[:, bass.ds(step.at(T), T), :]).then_inc(ctx_loaded[step.parity], 16)

            for p in WITH_CTX:
                for g in range(2):
                    if p == CROSS2:
                        sp.wait_ge(ctx_turned, cnt.at("ctx_turned", Step(CROSS, GROUPS - 2 + g)))
                    load_ctx(Step(p, g))
                with sp.Fori(0, GROUPS // 2 - 1) as turn:
                    for g in range(2):
                        sp.wait_ge(ctx_turned, cnt.at("ctx_turned", Step(p, g, turn)))
                        load_ctx(Step(p, g + 2, turn))
            o = out.rearrange("b n d -> (b n) d").rearrange("(t p) d -> p t d", p=ROWS)

            def store(step):
                sp.wait_ge(dve, cnt.at("dve", step, kind="down"))
                sp.dma_start(o[:, bass.ds(step.at(T), T), :],
                             row_slice(rows2, step, 0, T).rearrange("p (t d) -> p t d", d=D)).then_inc(stored, 16)

            with sp.Fori(0, GROUPS // 2 - 1) as turn:
                store(Step(FFN, 0, turn))
                store(Step(FFN, 1, turn))
            store(Step(FFN, GROUPS - 2))
            store(Step(FFN, GROUPS - 1))
            sp.wait_ge(stored, 16 * GROUPS)

        @block.tensor
        def _(pe):
            def stage_for(kind, step, i=0):
                n = cnt.uses.index((kind, step.phase, step.first, i))
                return n, stage[n % 3]

            def wait_stage(n, group):
                if group is not None:
                    into = n - cnt.start[("uses", group.phase, group.first)]
                    if into == 2:
                        pe.wait_ge(dve, cnt.start_of("dve", group))
                    if into < 3:
                        return
                elif n < 3:
                    return
                kind, p, g, i = cnt.uses[n - 3]
                turn = group.turn if group is not None else None
                a, v = copiers("up1" if kind == "up" and p == FFN else kind, i)
                if a:
                    pe.wait_ge(act, cnt.at("act", Step(p, g, turn), i, kind=kind))
                if v:
                    pe.wait_ge(dve, cnt.at("dve", Step(p, g, turn), i, kind=kind))

            def three(dst, weights, moving, start=True):
                (wh, wr), (mh, mr) = weights, moving
                nc.tensor.matmul(dst, wh, mh, start=start, stop=False)
                nc.tensor.matmul(dst, wh, mr, start=False, stop=False)
                return nc.tensor.matmul(dst, wr, mh, start=False, stop=True)

            def fold(p):
                s0 = Step(p, 0)
                pe.wait_ge(loaded_w[p], 64)
                for m, key in enumerate("kqv"):
                    k = C if p == CROSS and key != "q" else D
                    for c in range(2):
                        n, bank = stage_for("wt", s0, 2 * m + c)
                        wait_stage(n, None)
                        for q in range(4):
                            last = nc.tensor.transpose(bank[:, q * 128:q * 128 + k],
                                                       raw[key][0:k, (4 * c + q) * 128:(4 * c + q + 1) * 128],
                                                       ident[0:k, 0:k])
                        last.then_inc(full, 1)
                pe.wait_ge(act, cnt.at("act", s0, 4, kind="wt"))
                pe.wait_ge(dve, cnt.at("dve", s0, 5, kind="wt"))
                k = kdim[p]
                for i in range(4):
                    c, e = divmod(i, 2)
                    n, bank = stage_for("fa", s0, i)
                    wait_stage(n, None)
                    for q in range(4):
                        last = nc.tensor.matmul(bank[0:k, q * D:(q + 1) * D],
                                                turned_w["k"][64 * e:64 * e + 64, 4 * c + q, 0:k],
                                                turned_w["q"][64 * e:64 * e + 64, 4 * c + q, :], start=True, stop=True)
                    last.then_inc(full, 1)
                for i in range(4):
                    c, e = divmod(i, 2)
                    n, bank = stage_for("fb", s0, i)
                    wait_stage(n, None)
                    for q in range(4):
                        last = nc.tensor.matmul(bank[0:k, q * D:(q + 1) * D],
                                                turned_w["v"][64 * e:64 * e + 64, 4 * c + q, 0:k],
                                                raw["o"][64 * e:64 * e + 64, (4 * c + q) * D:(4 * c + q + 1) * D],
                                                start=True, stop=True)
                    last.then_inc(full, 1)

            def x_step(s, group):
                n, bank = stage_for("x", s)
                wait_stage(n, group)
                pe.wait_ge(normed, cnt.at("normed", s))
                if s.phase in WITH_CTX:
                    pe.wait_ge(ctx_loaded[s.parity], cnt.at(f"ctx{s.parity}", s))
                    for t in range(T):
                        last = nc.tensor.transpose(bank[0:C, GR + t * ROWS:GR + (t + 1) * ROWS],
                                                   ctx_in[s.parity][:, t, :], ident[:, :])
                    last.then_inc(ctx_turned, 1)
                for t in range(T):
                    last = nc.tensor.transpose(bank[:, t * ROWS:(t + 1) * ROWS], xn[:, t, :], ident[:, :])
                last.then_inc(full, 1)

            def p_step(s, group):
                par = s.parity
                if s.phase != CROSS2:
                    pe.wait_ge(rest, cnt.at("rest", s))
                if s.phase in (SELF, CROSS):
                    k = kdim[s.phase]
                    if s.phase == SELF and group is None:
                        pe.wait_ge(act, cnt.at("act", Step(SELF, 0), 3, kind="fb"))
                        pe.wait_ge(dve, cnt.at("dve", Step(SELF, 0), 3, kind="fb"))
                    for i in range(8):
                        n, bank = stage_for("k", s, i)
                        wait_stage(n, group)
                        for e in range(2):
                            last = three(bank[:, e * GR:(e + 1) * GR],
                                         [m[0:k, 2 * i + e, :] for m in fold_a[s.phase]],
                                         [m[0:k, :] for m in src[par]])
                        last.then_inc(full, 1)
                elif s.phase == CROSS2:
                    n, bank = stage_for("qk", s)
                    wait_stage(n, group)
                    nc.tensor.matmul(bank[:, 0:GR], wq1[:, :], xT[par][:, :], start=True, stop=True)
                    nc.tensor.matmul(bank[:, GR:2 * GR], wk1[:, :], cT[par][:, :], start=True, stop=True)\
                        .then_inc(full, 1)
                    n, bank = stage_for("v", s)
                    wait_stage(n, group)
                    for t in range(T):
                        last = nc.tensor.matmul(bank[:, t * D:(t + 1) * D], cT[par][:, t * ROWS:(t + 1) * ROWS],
                                                wv1[:, :], start=True, stop=True)
                    last.then_inc(full, 1)
                else:
                    if s.turn is None and s.first == 0:
                        pe.wait_ge(rest_w, 1 if s.phase == GEGLU else 2)
                    for i in range(4):
                        n, bank = stage_for("up", s, i)
                        wait_stage(n, group)
                        if s.phase == GEGLU:
                            three(bank[:, 0:GR], [m[:, i * 128:(i + 1) * 128] for m in wp_s], [m[:, :] for m in src[par]])
                            last = three(bank[:, GR:2 * GR], [m[:, FF + i * 128:FF + (i + 1) * 128] for m in wp_s],
                                         [m[:, :] for m in src[par]])
                        else:
                            last = three(bank[:, 0:GR], [m[:, i * 128:(i + 1) * 128] for m in w1_s],
                                         [m[:, :] for m in src[par]])
                        last.then_inc(full, 1)

            def scores_step(s):
                stat = qT if s.phase == CROSS2 else xT[s.parity]
                for t in range(T):
                    for c in range(2):
                        for b in range(2):
                            last = nc.tensor.matmul(scp[64 * b:64 * b + 64, 2 * t + c, :],
                                                    stat[:, (2 * t + b) * N:(2 * t + b + 1) * N],
                                                    kt[:, 2 * t + b, 8 * c:8 * c + 8, :], start=True, stop=True)
                    last.then_inc(scores, 1)

            def z_step(s):
                k = kdim[s.phase]
                for i in range(8):
                    t, e, c = i // 4, i // 2 % 2, i % 2
                    n, bank = stage_for("z", s, i)
                    wait_stage(n, s)
                    last = three(bank[:, :], [m[0:k, t * ROWS:(t + 1) * ROWS] for m in src[s.parity]],
                                 [m[0:k, e, 4 * c:4 * c + 4, :] for m in fold_b[s.phase]])
                    last.then_inc(full, 1)

            def turn_step(s, t):
                if s.phase == CROSS2:
                    pe.wait_ge(exped, cnt.at("exp", s, t))
                else:
                    pe.wait_ge(probs, cnt.at("probs", s, t))
                for c in range(2):
                    for q in range(4):
                        a = 4 * c + q
                        last = nc.tensor.transpose(scp[:, 2 * t + c, q * 128:(q + 1) * 128],
                                                   pr[t][:, a * 128:(a + 1) * 128], ident[:, :])
                    last.then_inc(turned, 1)

            def out_step(s, t):
                if t == 0:
                    bank, done = out0p, out0
                else:
                    n, bank = stage_for("out1", s)
                    wait_stage(n, s)
                    done = full
                pe.wait_ge(pt_act, cnt.at("pt_act", s, t))
                pe.wait_ge(pt_dve, cnt.at("pt_dve", s, t))
                if s.phase != CROSS2 and t == 0:
                    pe.wait_ge(act, cnt.at("act", s, 7, kind="z"))
                    pe.wait_ge(dve, cnt.at("dve", s, 7, kind="z"))
                for a in range(PAIRS):
                    for b in range(2):
                        if s.phase == CROSS2:
                            v = 2 * (H1 + 1)
                            last = nc.tensor.matmul(bank[64 * b:64 * b + 64, a * v:(a + 1) * v],
                                                    pt[t][:, a, 64 * b:64 * b + 64],
                                                    vb[s.parity][:, 2 * t + b, a, :], start=True, stop=True)
                        else:
                            last = nc.tensor.matmul(bank[64 * b:64 * b + 64, 0:D], pt[t][:, a, 64 * b:64 * b + 64],
                                                    zt[:, 2 * t + b, a, :], start=(a == 0), stop=(a == PAIRS - 1))
                last.then_inc(done, 1)

            def group(s):
                one, two = s.ahead(1), s.ahead(2)
                pe.wait_ge(act, cnt.start_of("act", s))
                pe.wait_ge(dve, cnt.start_of("dve", s) - 1)
                if s.phase in (SELF, CROSS, CROSS2):
                    if s.phase == CROSS2:
                        pe.wait_ge(masked, cnt.at("masked", s))
                    scores_step(s)
                    if one:
                        p_step(one, s)
                    if s.phase != CROSS2:
                        z_step(s)
                    turn_step(s, 0)
                    turn_step(s, 1)
                    if two:
                        x_step(two, s)
                    out_step(s, 0)
                    out_step(s, 1)
                    if s.phase == CROSS2:
                        n, bank = stage_for("at", s)
                        wait_stage(n, s)
                        pe.wait_ge(dve, cnt.at("dve", s, kind="out1"))
                        for t in range(T):
                            last = nc.tensor.transpose(bank[:, t * ROWS:(t + 1) * ROWS], att[:, t, :], ident[:, :])
                        last.then_inc(full, 1)
                        n, bank = stage_for("wo", s)
                        wait_stage(n, s)
                        pe.wait_ge(act, cnt.at("act", s, kind="at"))
                        for t in range(T):
                            last = nc.tensor.matmul(bank[:, t * D:(t + 1) * D], attT[:, t * ROWS:(t + 1) * ROWS],
                                                    wo1[:, :], start=True, stop=True)
                        last.then_inc(full, 1)
                else:
                    if one:
                        p_step(one, s)
                    if two:
                        x_step(two, s)
                    n, bank = stage_for("down", s)
                    wait_stage(n, s)
                    wd = wf if s.phase == GEGLU else w2
                    for t in range(T):
                        for i in range(FF // 128):
                            last = nc.tensor.matmul(bank[:, t * D:(t + 1) * D],
                                                    hid[s.parity][:, i, t * ROWS:(t + 1) * ROWS], wd[:, i, :],
                                                    start=(i == 0), stop=(i == FF // 128 - 1))
                    last.then_inc(full, 1)

            pe.wait_ge(made_ident, 2)
            fold(SELF)
            fold(CROSS)
            x_step(Step(SELF, 0), None)
            p_step(Step(SELF, 0), None)
            x_step(Step(SELF, 1), None)
            pe.wait_ge(loaded_ffn, 16 * 8)
            each_group(pe, group)

        @block.scalar
        def _(sc):
            names = {G1: "L0_xattn_g1", B1_: "L0_xattn_b1", G2: "L0_xattn_g2", B2_: "L0_xattn_b2", G3: "L0_xattn_g3",
                     B3_: "L0_xattn_b3", G4: "L1_xattn_ln_g", B4_: "L1_xattn_ln_b", BQ: "L1_xattn_bq", BK: "L1_xattn_bk",
                     BP: "L0_xattn_bp", BF1: "L1_xattn_b1"}
            with nc.allow_non_contiguous_dma(reason="vectors of at most 1024 values"):
                for c0, name in names.items():
                    v = w[name].rearrange("(c p) -> p c", p=128)
                    sc.dma_start(cols[:, c0:c0 + v.shape[1]], v).then_inc(loaded_small, 16)
            for c0, name in {BO1: "L0_xattn_bo1", BO2: "L0_xattn_bo2", BFF: "L0_xattn_bf", BO3: "L1_xattn_bo",
                             BV: "L1_xattn_bv", BLAST: "L1_xattn_b2"}.items():
                sc.dma_start(bias[:, c0, :], w[name][None, :].to_broadcast([128, D])).then_inc(loaded_small, 16)

            def copy(dst, s):
                return nc.scalar.activation(dst, s, ACT.Copy)

            def fold(p):
                s0, k = Step(p, 0), kdim[p]
                for m, key in enumerate("kqv"):
                    kk = k if key != "q" else D
                    sc.wait_ge(full, cnt.at("full", s0, 2 * m, kind="wt"))
                    bank = stage[cnt.bank("wt", s0, 2 * m)]
                    copy(turned_w[key][:, 0:4, 0:kk],
                         bank[:, :].rearrange("p (q k) -> p q k", q=4)[:, :, 0:kk]).then_inc(act, 1)
                for kind, dst in (("fa", fold_a[p]), ("fb", fold_b[p])):
                    for i in range(4):
                        c, e = divmod(i, 2)
                        sc.wait_ge(full, cnt.at("full", s0, i, kind=kind))
                        bank = stage[cnt.bank(kind, s0, i)]
                        copy(parts(kind, dst[0], c, e, k),
                             bank[0:k, :].rearrange("p (q d) -> p q d", q=4)).then_inc(act, 1)

            def x_step(s):
                if s.phase == CROSS2:
                    return
                k = C if s.phase == CROSS else D
                sc.wait_ge(dve, cnt.at("dve", s, kind="x"))
                copy(src[s.parity][0][0:k, :], (cT if s.phase == CROSS else xT)[s.parity][:, :]).then_inc(high, 1)

            def p_step(s, which=None):
                par = s.parity
                if s.phase in (SELF, CROSS):
                    for i in which:
                        if i in K_BY_DVE:
                            continue
                        sc.wait_ge(full, cnt.at("full", s, i, kind="k"))
                        copy(*key_copy(s, i)).then_inc(act, 1)
                elif s.phase == CROSS2:
                    sc.wait_ge(full, cnt.at("full", s, kind="qk"))
                    bank = stage[cnt.bank("qk", s)]
                    nc.scalar.activation(qT[:, :], bank[:, 0:GR], ACT.Identity, bias=cols[:, BQ:BQ + 1])
                    nc.scalar.activation(kT[:, :], bank[:, GR:2 * GR], ACT.Identity, bias=cols[:, BK:BK + 1])\
                        .then_inc(act, 1)
                else:
                    for i in range(4):
                        sc.wait_ge(full, cnt.at("full", s, i, kind="up"))
                        bank = stage[cnt.bank("up", s, i)]
                        if s.phase == GEGLU:
                            if i >= 2:
                                sc.wait_ge(dve, cnt.at("dve", s, i - 2, kind="up"))
                            nc.scalar.activation(ge[i % 2][:, :], bank[:, GR:2 * GR], ACT.Gelu,
                                                 bias=cols[:, BP + 4 + i:BP + 5 + i]).then_inc(gelued, 1)
                        else:
                            nc.scalar.activation(hid[par][:, i, :], bank[:, 0:GR], ACT.Gelu,
                                                 bias=cols[:, BF1 + i:BF1 + i + 1]).then_inc(act, 1)

            def exp_step(s, t):
                sc.wait_ge(shifted, cnt.at("shifted", s, t))
                nc.scalar.activation(pr[t][:, :], pr[t][:, :], ACT.Exp, scale=scale[s.phase]).then_inc(exped, 1)

            def group(s):
                one, two = s.ahead(1), s.ahead(2)
                if s.phase in (SELF, CROSS, CROSS2):
                    exp_step(s, 0)
                    if one and one.phase in (SELF, CROSS):
                        p_step(one, range(3))
                        exp_step(s, 1)
                        p_step(one, range(3, 8))
                    elif one and one.phase == CROSS2:
                        p_step(one)
                        exp_step(s, 1)
                    else:
                        exp_step(s, 1)
                        if one:
                            p_step(one)
                    if s.phase != CROSS2:
                        for i in range(8):
                            sc.wait_ge(full, cnt.at("full", s, i, kind="z"))
                            for b in range(2 if i in Z_BY_ACT else 1):
                                copy(*value_copy(s, i, b)).then_inc(act, 1)
                    for t in range(T):
                        sc.wait_ge(turned, cnt.at("turned", s, t, 0))
                        copy(pt[t][:, 0:4, :], scp[:, 2 * t, :].rearrange("p (q n) -> p q n", q=4)).then_inc(pt_act, 1)
                    if two:
                        x_step(two)
                    if s.phase == CROSS2:
                        sc.wait_ge(full, cnt.at("full", s, kind="at"))
                        copy(attT[:, :], stage[cnt.bank("at", s)][:, 0:GR]).then_inc(act, 1)
                else:
                    if one:
                        p_step(one)
                    if two:
                        x_step(two)

            sc.wait_ge(loaded_small, 16 * 18)
            fold(SELF)
            fold(CROSS)
            sc.wait_ge(loaded_ffn, 16 * 8)
            copy(wp_s[0][:, :], wp[:, :]).then_inc(high_w, 1)
            copy(w1_s[0][:, :], w1[:, :]).then_inc(high_w, 1)
            x_step(Step(SELF, 0))
            p_step(Step(SELF, 0), range(8))
            x_step(Step(SELF, 1))
            each_group(sc, group)

        @block.vector
        def _(ve):
            def fold(p):
                s0, k = Step(p, 0), kdim[p]
                for m, key in enumerate("kqv"):
                    kk = k if key != "q" else D
                    ve.wait_ge(full, cnt.at("full", s0, 2 * m + 1, kind="wt"))
                    bank = stage[cnt.bank("wt", s0, 2 * m + 1)]
                    nc.vector.tensor_copy(turned_w[key][:, 4:8, 0:kk],
                                          bank[:, :].rearrange("p (q k) -> p q k", q=4)[:, :, 0:kk]).then_inc(dve, 1)
                for kind, dst in (("fa", fold_a[p]), ("fb", fold_b[p])):
                    for i in range(4):
                        c, e = divmod(i, 2)
                        ve.wait_ge(act, cnt.at("act", s0, i, kind=kind))
                        bank = stage[cnt.bank(kind, s0, i)]
                        nc.vector.tensor_tensor(parts(kind, dst[1], c, e, k),
                                                bank[0:k, :].rearrange("p (q d) -> p q d", q=4),
                                                parts(kind, dst[0].bitcast(F32), c, e, k), ALU.subtract).then_inc(dve, 1)

            def stats_step(s):
                if s.phase == CROSS2:
                    return
                buf = rows2 if s.phase == FFN else rows
                for t in range(T):
                    last = nc.vector.bn_stats(stats[s.parity][:, t, :], row_slice(buf, s, t))
                last.then_inc(stated, 1)
                ve.wait_ge(stated, cnt.at("stats", s))
                nc.vector.tensor_copy(seen[:, :], stats[s.parity][:, T - 1, 0:1])
                for t in range(T):
                    last = nc.vector.bn_aggr(mv[s.parity][:, t, :], stats[s.parity][:, t, :])
                last.then_inc(meaned, 1)

            def norm_step(s):
                if s.phase == CROSS2:
                    nc.vector.tensor_copy(xn[:, :, :], row_slice(rows, s, 0, T).rearrange("p (t d) -> p t d", t=T))\
                        .then_inc(normed, 1)
                    return
                ve.wait_ge(rooted, cnt.at("rstd", s))
                buf = rows2 if s.phase == FFN else rows
                for t in range(T):
                    last = nc.vector.tensor_scalar(xn[:, t, :], row_slice(buf, s, t), mv[s.parity][:, t, 0:1],
                                                   rstd[s.parity][:, t:t + 1], ALU.subtract, ALU.mult)
                last.then_inc(normed, 1)

            def x_step(s):
                ve.wait_ge(full, cnt.at("full", s, kind="x"))
                bank = stage[cnt.bank("x", s)]
                if s.phase == CROSS2:
                    last = nc.vector.tensor_copy(xT[s.parity][:, :], bank[:, 0:GR])
                else:
                    g = {SELF: G1, CROSS: G2, GEGLU: G3, FFN: G4}[s.phase]
                    last = nc.vector.tensor_scalar(xT[s.parity][:, :], bank[:, 0:GR], cols[:, g:g + 1],
                                                   cols[:, g + 1:g + 2], ALU.mult, ALU.add)
                if s.phase in WITH_CTX:
                    last = nc.vector.tensor_copy(cT[s.parity][:, :], bank[0:C, GR:2 * GR])
                last.then_inc(dve, 1)

            def p_step(s):
                par = s.parity
                if s.phase in (SELF, CROSS):
                    for i in K_BY_DVE:
                        ve.wait_ge(full, cnt.at("full", s, i, kind="k"))
                        nc.vector.tensor_copy(*key_copy(s, i)).then_inc(dve, 1)
                elif s.phase == CROSS2:
                    ve.wait_ge(full, cnt.at("full", s, kind="v"))
                    bank = stage[cnt.bank("v", s)]
                    for t in range(T):
                        for b in range(2):
                            for e in range(2):
                                h = slice(64 * b, 64 * b + 64)
                                v = bank[h, t * D:(t + 1) * D].rearrange("p (a e d) -> p a e d", e=2, d=H1)[:, :, e, :]
                                vv = bias[h, BV, :].rearrange("p (a e d) -> p a e d", e=2, d=H1)[:, :, e, :]
                                last = nc.vector.tensor_tensor(
                                    vb[par][64 * e:64 * e + 64, 2 * t + b, :, e * (H1 + 1):e * (H1 + 1) + H1],
                                    v, vv, ALU.add)
                    last.then_inc(dve, 1)
                elif s.phase == GEGLU:
                    for i in range(4):
                        ve.wait_ge(gelued, cnt.at("gelu", s, i))
                        bank = stage[cnt.bank("up", s, i)]
                        nc.vector.scalar_tensor_tensor(hid[par][:, i, :], bank[:, 0:GR], cols[:, BP + i:BP + i + 1],
                                                       ge[i % 2][:, :], op0=ALU.add, op1=ALU.mult).then_inc(dve, 1)

            def max_step(s, t):
                ve.wait_ge(scores, cnt.at("scores", s, t))
                sc3 = scp[:, 2 * t:2 * t + 2, :].rearrange("p c (h n) -> p (c h) n", n=N)
                nc.vector.tensor_reduce(mx[:, t, :], sc3, AX.X, ALU.max).then_inc(maxed, 1)
                ve.wait_ge(maxed, cnt.at("max", s, t))
                nc.vector.tensor_tensor(halves(pr[t][:, :]), sc3, mx[:, t, :, None].to_broadcast([ROWS, H, N]),
                                        ALU.subtract).then_inc(shifted, 1)

            def sum_step(s, t):
                ve.wait_ge(exped, cnt.at("exp", s, t))
                nc.vector.tensor_reduce(sm[:, t, :], halves(pr[t][:, :]), AX.X, ALU.add).then_inc(summed, 1)
                ve.wait_ge(summed, cnt.at("sums", s, t))
                nc.vector.reciprocal(rc[:, t, :], sm[:, t, :]).then_inc(recip, 1)

            def out_step(s, t):
                if t == 0:
                    ve.wait_ge(out0, cnt.at("out0", s))
                    bank = out0p
                else:
                    ve.wait_ge(full, cnt.at("full", s, kind="out1"))
                    bank = stage[cnt.bank("out1", s)]
                if s.phase == CROSS2:
                    o = bank[:, 0:H * (H1 + 1)].rearrange("p (h v) -> p h v", v=H1 + 1)
                    nc.vector.reciprocal(rc[:, t, :, None], o[:, :, H1:H1 + 1]).then_inc(normr, 1)
                    ve.wait_ge(normr, cnt.at("norm", s, t))
                    last = nc.vector.tensor_tensor(att[:, t, :].rearrange("p (h v) -> p h v", v=H1), o[:, :, 0:H1],
                                                   rc[:, t, :, None].to_broadcast([ROWS, H, H1]), ALU.mult)
                    if t == 1:
                        last.then_inc(dve, 1)
                else:
                    r = row_slice(rows, s, t)
                    last = nc.vector.tensor_tensor(r, bank[:, 0:D], r, ALU.add)
                    if t == 1:
                        last.then_inc(dve, 1)

            def group(s):
                one, two = s.ahead(1), s.ahead(2)
                if two:
                    stats_step(two)
                if s.phase in (SELF, CROSS, CROSS2):
                    max_step(s, 0)
                    max_step(s, 1)
                    if two:
                        norm_step(two)
                    if one:
                        p_step(one)
                    if s.phase != CROSS2:
                        sum_step(s, 0)
                        sum_step(s, 1)
                        for i in range(8):
                            if i not in Z_BY_ACT:
                                ve.wait_ge(full, cnt.at("full", s, i, kind="z"))
                                nc.vector.tensor_copy(*value_copy(s, i, 1)).then_inc(dve, 1)
                    for t in range(T):
                        ve.wait_ge(turned, cnt.at("turned", s, t, 1))
                        nc.vector.tensor_copy(pt[t][:, 4:8, :],
                                              scp[:, 2 * t + 1, :].rearrange("p (q n) -> p q n", q=4)).then_inc(pt_dve, 1)
                    if two:
                        x_step(two)
                    out_step(s, 0)
                    out_step(s, 1)
                    if s.phase == CROSS2:
                        ve.wait_ge(full, cnt.at("full", s, kind="wo"))
                        bank = stage[cnt.bank("wo", s)]
                        nc.vector.tensor_tensor(row_slice(rows2, s, 0, T).rearrange("p (t d) -> p t d", t=T),
                                                bank[:, 0:GR].rearrange("p (t d) -> p t d", t=T),
                                                bias[:, None, BO3, :].to_broadcast([ROWS, T, D]), ALU.add).then_inc(dve, 1)
                else:
                    if two:
                        norm_step(two)
                    if one:
                        p_step(one)
                    if two:
                        x_step(two)
                    ve.wait_ge(full, cnt.at("full", s, kind="down"))
                    ve.wait_ge(biased, cnt.at("biased", s))
                    bank = stage[cnt.bank("down", s)]
                    r = row_slice(rows if s.phase == GEGLU else rows2, s, 0, T)
                    nc.vector.tensor_tensor(r, bank[:, 0:GR], r, ALU.add).then_inc(dve, 1)

            fold(SELF)
            fold(CROSS)
            ve.wait_ge(loaded_rows, 64)
            ve.wait_ge(loaded_small, 16 * 18)
            stats_step(Step(SELF, 0))
            norm_step(Step(SELF, 0))
            x_step(Step(SELF, 0))
            stats_step(Step(SELF, 1))
            p_step(Step(SELF, 0))
            norm_step(Step(SELF, 1))
            x_step(Step(SELF, 1))
            each_group(ve, group)

        @block.gpsimd
        def _(gp):
            nc.gpsimd.memset(ident[:, :], 0.0).then_inc(made_ident, 1)
            gp.wait_ge(made_ident, 1)
            nc.gpsimd.affine_select(out=ident[:, :], in_=ident[:, :], compare_op=ALU.not_equal, fill=1.0, base=0,
                                    pattern=[[-1, 128]], channel_multiplier=1).then_inc(made_ident, 1)
            nc.gpsimd.memset(neghalf[:, :], -0.5).then_inc(made_half, 1)
            nc.gpsimd.memset(eps[:, :], EPS).then_inc(made_half, 1)
            nc.gpsimd.memset(headmask[:, :], 1.0).then_inc(made_mask, 1)
            gp.wait_ge(made_mask, 1)
            nc.gpsimd.affine_select(out=headmask[:, :], in_=headmask[:, :], compare_op=ALU.is_ge, fill=0.0, base=0,
                                    pattern=[[-H1, H]], channel_multiplier=1).then_inc(made_mask, 1)
            gp.wait_ge(made_mask, 2)
            nc.gpsimd.affine_select(out=headmask[:, :], in_=headmask[:, :], compare_op=ALU.is_ge, fill=0.0, base=H1 - 1,
                                    pattern=[[H1, H]], channel_multiplier=-1).then_inc(made_mask, 1)
            for n in range(2):
                nc.gpsimd.memset(vb[n][:, :, :, :], 0.0).then_inc(made_vb, 1)
            gp.wait_ge(made_vb, 2)
            for n in range(2):
                for e in range(2):
                    one = (e + 1) * (H1 + 1) - 1
                    nc.gpsimd.memset(vb[n][64 * e:64 * e + 64, :, :, one:one + 1], 1.0).then_inc(made_vb, 1)

            def rstd_step(s):
                if s.phase == CROSS2:
                    return
                gp.wait_ge(meaned, cnt.at("mean", s))
                nc.gpsimd.tensor_tensor(veps[:, :], mv[s.parity][:, :, 1], eps[:, :], ALU.add).then_inc(epsed, 1)
                gp.wait_ge(epsed, cnt.at("eps", s))
                nc.gpsimd.tensor_tensor(rstd[s.parity][:, :], veps[:, :], neghalf[:, :], ALU.pow).then_inc(rooted, 1)

            def bias_step(s):
                if s.phase == CROSS2:
                    return
                gp.wait_ge(normed, cnt.at("normed", s))
                buf = rows2 if s.phase == FFN else rows
                r = row_slice(buf, s, 0, T)
                r3 = r.rearrange("p (t d) -> p t d", t=T)
                b = {SELF: BO1, CROSS: BO2, GEGLU: BFF, FFN: BLAST}[s.phase]
                nc.gpsimd.tensor_tensor(r3, r3, bias[:, None, b, :].to_broadcast([ROWS, T, D]), ALU.add)\
                    .then_inc(biased, 1)
                if s.phase == FFN:
                    gp.wait_ge(biased, cnt.at("biased", s))
                    nc.gpsimd.tensor_tensor(r, r, row_slice(rows, s, 0, T), ALU.add).then_inc(summed2, 1)

            def rest_step(s):
                if s.phase == CROSS2:
                    return
                k = C if s.phase == CROSS else D
                gp.wait_ge(high, cnt.at("high", s))
                hp, rp = src[s.parity]
                nc.gpsimd.tensor_tensor(rp[0:k, :], (cT if s.phase == CROSS else xT)[s.parity][:, :],
                                        hp.bitcast(F32)[0:k, :], ALU.subtract).then_inc(rest, 1)

            def mask_step(s):
                gp.wait_ge(act, cnt.at("act", s, kind="qk"))
                for b in range(GB):
                    last = nc.gpsimd.tensor_tensor(kt[:, b, :, :],
                                                   kT[:, None, b * N:(b + 1) * N].to_broadcast([D, H, N]),
                                                   headmask[:, :, None].to_broadcast([D, H, N]), ALU.mult)
                last.then_inc(masked, 1)

            def group(s):
                one, two = s.ahead(1), s.ahead(2)
                if two:
                    rstd_step(two)
                    bias_step(two)
                if s.phase in (SELF, CROSS):
                    for t in range(T):
                        gp.wait_ge(recip, cnt.at("recip", s, t))
                        nc.gpsimd.tensor_tensor(halves(pr[t][:, :]), halves(pr[t][:, :]),
                                                rc[:, t, :, None].to_broadcast([ROWS, H, N]), ALU.mult).then_inc(probs, 1)
                if one and one.phase == CROSS2:
                    mask_step(one)
                if two:
                    rest_step(two)

            gp.wait_ge(loaded_small, 16 * 18)
            gp.wait_ge(made_half, 2)
            gp.wait_ge(made_mask, 3)
            gp.wait_ge(made_vb, 6)
            for g in range(2):
                rstd_step(Step(SELF, g))
                bias_step(Step(SELF, g))
                rest_step(Step(SELF, g))
            for n, (whole, s) in enumerate(((wp, wp_s), (w1, w1_s))):
                gp.wait_ge(high_w, n + 1)
                nc.gpsimd.tensor_tensor(s[1][:, :], whole[:, :], s[0].bitcast(F32)[:, :], ALU.subtract).then_inc(rest_w, 1)
            each_group(gp, group)


_OUTS = [((B, N, D), "float32")]


def kernel(**inputs):
    import numpy as _np
    import concourse.bacc as _bacc
    from concourse import mybir as _mybir
    from concourse.bass_utils import run_bass_kernel_spmd as _run

    nc = _bacc.Bacc("TRN2", target_bir_lowering=False, num_devices=1)
    arrays, aps = {}, {}
    for name, value in inputs.items():
        a = _np.ascontiguousarray(value)
        arrays[f"in_{name}_dram"] = a
        aps[name] = nc.dram_tensor(f"in_{name}_dram", a.shape, _mybir.dt.from_np(a.dtype), kind="ExternalInput").ap()
    outs = [nc.dram_tensor(f"out_{i}_dram", shape, _mybir.dt.from_np(_np.dtype(dtype)), kind="ExternalOutput").ap()
            for i, (shape, dtype) in enumerate(_OUTS)]
    attention_blocks(nc, aps, outs[0])
    r = _run(nc, [arrays], core_ids=[0])
    return r.results[0]["out_0_dram"]
```

```python
import concourse.bass as bass
from concourse import mybir
from contextlib import ExitStack

F32 = mybir.dt.float32
F32R = mybir.dt.float32r
ACT = mybir.ActivationFunctionType
ALU = mybir.AluOpType
AX = mybir.AxisListType

B, N, D, C = 32, 64, 128, 96
H, DH = 16, 64
H1 = D // H
FF = 4 * D
EPS = 1e-5
ROWS = 128
TILES = B * N // ROWS
T = 2
GB = T * ROWS // N
GR = T * ROWS
GROUPS = TILES // T
PAIRS = H // 2
BANK = 512
SELF, CROSS, GEGLU, CROSS2, FFN = range(5)
PHASES = 5
WITH_CTX = (CROSS, CROSS2)

K_BY_DVE = (5, 6)
Z_BY_ACT = (0,)


def copiers(kind, i):
    if kind in ("fa", "fb"):
        return 1, 1
    if kind == "wt":
        return (1, 0) if i % 2 == 0 else (0, 1)
    if kind == "k":
        return (0, 1) if i in K_BY_DVE else (1, 0)
    if kind == "z":
        return (2, 0) if i in Z_BY_ACT else (1, 1)
    if kind in ("x", "qk", "at", "up1"):
        return 1, 0
    return 0, 1


class Step:

    def __init__(self, phase, first, turn=None, turns=1):
        self.phase, self.first, self.turn, self.turns = phase, first, turn, turns
        self.parity = first % 2

    def ahead(self, k):
        if self.first + k < GROUPS:
            return Step(self.phase, self.first + k, self.turn, self.turns)
        assert self.turn is None
        return Step(self.phase + 1, self.first + k - GROUPS) if self.phase + 1 < PHASES else None

    def before(self):
        return Step(self.phase, self.first - 1, self.turn, self.turns) if self.first > 0 else None

    def at(self, scale, offset=0):
        if self.turn is None:
            return self.first * scale + offset
        return self.turn * (2 * scale) + (self.first * scale + offset)


class Counts:

    def __init__(self):
        self.total, self.value, self.uses, self.start = {}, {}, [], {}
        self.fold(SELF)
        self.x(SELF, 0)
        self.x(SELF, 1)
        self.fold(CROSS)
        self.p(SELF, 0)
        for p in range(PHASES):
            for g in range(GROUPS):
                self.group(p, g)

    def tick(self, name, key, n=1):
        self.total[name] = self.total.get(name, 0) + n
        self.value[(name, *key)] = self.total[name]

    def use(self, kind, p, g, i=0):
        self.tick("full", (kind, p, g, i))
        for name, n in zip(("act", "dve"), copiers("up1" if kind == "up" and p == FFN else kind, i)):
            self.tick(name, (kind, p, g, i), n)
        self.uses.append((kind, p, g, i))

    def fold(self, p):
        for kind, n in (("wt", 6), ("fa", 4), ("fb", 4)):
            for i in range(n):
                self.use(kind, p, 0, i)

    def x(self, p, g):
        if p != CROSS2:
            for name in ("stats", "mean", "rstd", "biased"):
                self.tick(name, (p, g))
            if p == FFN:
                self.tick("summed2", (p, g))
        self.tick("normed", (p, g))
        if p != CROSS2:
            self.tick("high", (p, g))
            self.tick("rest", (p, g))
        if p in WITH_CTX:
            self.tick(f"ctx{g % 2}", (p, g), 16)
            self.tick("ctx_turned", (p, g))
        self.use("x", p, g)

    def p(self, p, g, which=range(4)):
        for kind, n in {SELF: [("k", 8)], CROSS: [("k", 8)], CROSS2: [("qk", 1), ("v", 1)]}.get(p, [("up", 4)]):
            for i in which if kind == "up" else range(n):
                self.use(kind, p, g, i)
                if kind == "up" and p == GEGLU:
                    self.tick("gelu", (p, g, i))
        if p == CROSS2:
            for t in range(T):
                self.tick("masked", (p, g, t))

    def group(self, p, g):
        self.start[("act", p, g)] = self.total["act"]
        self.start[("dve", p, g)] = self.total["dve"]
        self.start[("uses", p, g)] = len(self.uses)
        one, two = Step(p, g).ahead(1), Step(p, g).ahead(2)
        if p in (SELF, CROSS):
            for t in range(T):
                self.softmax(p, g, t)
            if one.phase != GEGLU:
                self.p(one.phase, one.first)
            for t in range(T):
                for i in range(4):
                    self.use("z", p, g, 4 * t + i)
                self.turned(p, g, t)
                if t == 0:
                    self.tick("out0", (p, g))
            if one.phase == GEGLU:
                self.p(one.phase, one.first)
            self.x(two.phase, two.first)
            self.use("out1", p, g)
        elif p == CROSS2:
            if one.phase == CROSS2:
                self.p(one.phase, one.first)
            self.softmax(p, g, 1)
            if g > 0:
                self.finish(p, g - 1)
            self.turned(p, g, 0)
            if one.phase == CROSS2:
                self.x(two.phase, two.first)
            self.tick("out0", (p, g))
            self.turned(p, g, 1)
            if one.phase == CROSS2:
                self.softmax(one.phase, one.first, 0)
            self.use("out1", p, g)
            for t in range(T):
                self.tick("norm", (p, g, t))
            if one.phase != CROSS2:
                self.x(two.phase, two.first)
                self.p(one.phase, one.first)
                self.finish(p, g)
        else:
            if one:
                self.p(one.phase, one.first, range(3))
            if two:
                self.x(two.phase, two.first)
            if one and one.phase == p:
                self.p(one.phase, one.first, (3,))
            self.use("down", p, g)
            if one and one.phase == CROSS2:
                self.softmax(one.phase, one.first, 0)

    def softmax(self, p, g, t):
        for name in ("scores", "max", "shifted", "exp"):
            self.tick(name, (p, g, t))
        if p != CROSS2:
            for name in ("sums", "recip", "probs"):
                self.tick(name, (p, g, t))

    def turned(self, p, g, t):
        for c in range(2):
            self.tick("turned", (p, g, t, c))
        if p == CROSS2:
            for c in range(2):
                self.tick("pt_act", (p, g, t, c))
        else:
            self.tick("pt_act", (p, g, t, 0))
            self.tick("pt_dve", (p, g, t))

    def finish(self, p, g):
        self.use("at", p, g)
        self.use("wo", p, g)

    def linear(self, of, step):
        v = of(step.first)
        if step.turn is None:
            return v
        per = of(step.first + 2) - v
        for n in range(1, step.turns):
            assert of(step.first + 2 * n) == v + n * per, step
        return step.turn * per + v

    def at(self, name, step, *rest, kind=None):
        head = (name,) if kind is None else (name, kind)
        tail = rest if kind is None else (rest or (0,))
        return self.linear(lambda g: self.value[(*head, step.phase, g, *tail)], step)

    def start_of(self, name, step):
        return self.linear(lambda g: self.start[(name, step.phase, g)], step)

    def bank(self, kind, step, i=0):
        return self.uses.index((kind, step.phase, step.first, i)) % 3


def attention_blocks(nc, w, out):
    cnt = Counts()
    ctx = ExitStack()
    with ctx:
        def sb(name, shape, dt=F32):
            return ctx.enter_context(nc.sbuf_tensor(name, shape, dt))

        def ps(name, shape):
            return ctx.enter_context(nc.psum_tensor(name, shape, F32))

        def sem(name):
            return ctx.enter_context(nc.semaphore(name))

        rows = sb("rows", [ROWS, TILES * D])
        rows2 = sb("rows2", [ROWS, TILES * D])
        ident = sb("ident", [128, 128])
        headmask = sb("headmask", [128, H])
        fold_a = [[sb(f"fold_a{p}{n}", [128, H, D], F32R) for n in "hr"] for p in (SELF, CROSS)]
        fold_b = [[sb(f"fold_b{p}{n}", [128, 2, PAIRS, D], F32R) for n in "hr"] for p in (SELF, CROSS)]
        wp = sb("wp", [D, 2 * FF])
        wp_s = [sb(f"wp_{n}", [D, 2 * FF], F32R) for n in "hr"]
        w1 = sb("w1", [D, FF])
        w1_s = [sb(f"w1_{n}", [D, FF], F32R) for n in "hr"]
        wf = sb("wf", [128, FF // 128, D])
        w2 = sb("w2", [128, FF // 128, D])
        wq1, wo1 = sb("wq1", [D, D]), sb("wo1", [D, D])
        wk1, wv1 = sb("wk1", [C, D]), sb("wv1", [C, D])
        cols = sb("cols", [128, 22])
        bias = sb("bias", [128, 6, D])
        neghalf = sb("neghalf", [128, T])
        seen, seen_act = sb("seen", [ROWS, 1]), sb("seen_act", [ROWS, 1])
        ctx_in = [sb(f"ctx_in{n}", [ROWS, T, C]) for n in range(2)]
        stats = [sb(f"stats{n}", [128, T, 6]) for n in range(2)]
        mv = [sb(f"mv{n}", [128, T, 2]) for n in range(2)]
        veps = [sb(f"veps{n}", [128, T]) for n in range(2)]
        rstd = [sb(f"rstd{n}", [128, T]) for n in range(2)]
        xn = sb("xn", [ROWS, T, D])
        xT = [sb(f"xT{n}", [D, GR]) for n in range(2)]
        cT = [sb(f"cT{n}", [C, GR]) for n in range(2)]
        src = [[sb(f"src{n}{m}", [D, GR], F32R) for m in "hr"] for n in range(2)]
        kt = sb("kt", [D, GB, H, N])
        zt = sb("zt", [128, GB, PAIRS, D])
        pr = [sb(f"pr{t}", [ROWS, H * N]) for t in range(T)]
        mx = sb("mx", [ROWS, T, H])
        sm = sb("sm", [ROWS, T, H])
        rc = sb("rc", [ROWS, T, H])
        pt = [sb(f"pt{t}", [128, PAIRS, ROWS]) for t in range(T)]
        raw = {SELF: {k: zt[:, n, :, :].rearrange("p a d -> p (a d)") for n, k in enumerate("kqvo")},
               CROSS: dict(zip("kqvo", (pr[0][:, :], pr[1][:, :], *(b[:, :, :].rearrange("p a n -> p (a n)") for b in pt))))}
        turned_w = {k: kt[:, n, :, :].rearrange("p h n -> p (h n)").rearrange("p (a k) -> p a k", k=128)
                    for n, k in enumerate("kqv")}
        ge = [sb(f"ge{n}", [128, GR]) for n in range(2)]
        hid = [sb(f"hid{n}", [128, FF // 128, GR]) for n in range(2)]
        qT, kT = ([sb(f"{m}T{n}", [D, GR]) for n in range(2)] for m in "qk")
        vb = [sb(f"vb{n}", [128, GB, PAIRS, 2 * (H1 + 1)]) for n in range(2)]
        att = sb("att", [ROWS, T, D])
        attT = sb("attT", [D, GR])

        G1, B1_, G2, B2_, G3, B3_, G4, B4_ = range(8)
        BQ, BK, BP, BF1 = 8, 9, 10, 18
        BO1, BO2, BFF, BO3, BV, BLAST = range(6)
        BIAS = 100
        FIRST_VECTORS = {G1: "L0_xattn_g1", B1_: "L0_xattn_b1", BIAS + BO1: "L0_xattn_bo1"}
        VECTORS = {G2: "L0_xattn_g2", B2_: "L0_xattn_b2", G3: "L0_xattn_g3", B3_: "L0_xattn_b3", G4: "L1_xattn_ln_g",
                   B4_: "L1_xattn_ln_b", BQ: "L1_xattn_bq", BK: "L1_xattn_bk", BP: "L0_xattn_bp", BF1: "L1_xattn_b1",
                   BIAS + BO2: "L0_xattn_bo2", BIAS + BFF: "L0_xattn_bf", BIAS + BO3: "L1_xattn_bo",
                   BIAS + BV: "L1_xattn_bv", BIAS + BLAST: "L1_xattn_b2"}

        scp = ps("scp", [128, 4, BANK])
        stage = [ps(f"stage{n}", [128, BANK]) for n in range(3)]
        out0p = ps("out0p", [128, BANK])

        full = sem("stage_full")
        act = sem("stage_copied_act")
        dve = sem("stage_copied_dve")
        scores = sem("scores")
        maxed = sem("maxed")
        shifted = sem("shifted")
        exped = sem("exped")
        summed = sem("summed")
        recip = sem("recip")
        probs = sem("probs")
        turned = sem("turned")
        pt_act = sem("pt_act")
        pt_dve = sem("pt_dve")
        out0 = sem("out0")
        stated = sem("stated")
        meaned = sem("meaned")
        epsed = sem("epsed")
        rooted = sem("rooted")
        normed = sem("normed")
        biased = sem("biased")
        summed2 = sem("summed2")
        high = sem("high")
        rest = sem("rest")
        ctx_loaded = [sem("ctx_loaded0"), sem("ctx_loaded1")]
        ctx_turned = sem("ctx_turned")
        gelued = sem("gelued")
        masked = sem("masked")
        masked_dve = sem("masked_dve")
        normr = sem("normr")
        loaded_rows = [sem("loaded_rows0"), sem("loaded_rows1")]
        loaded_w = [{k: sem(f"loaded_w{k}{p}") for k in "kqvo"} for p in (SELF, CROSS)]
        loaded_first = sem("loaded_first")
        loaded_small = sem("loaded_small")
        loaded_ffn = sem("loaded_ffn")
        made_ident = sem("made_ident")
        made_mask = sem("made_mask")
        made_half = sem("made_half")
        made_vb = sem("made_vb")
        high_w = sem("high_w")
        rest_w = sem("rest_w")
        stored = sem("stored")

        scale = {SELF: DH ** -0.5, CROSS: DH ** -0.5, CROSS2: H1 ** -0.5}
        kdim = {SELF: D, CROSS: C}

        def row_slice(buf, step, t=0, n=1):
            return buf[:, bass.ds(step.at(T * D, t * D), n * D)]

        def each_group(eng, body, far=False):
            for p in range(PHASES):
                lead, tail = (2 if p == CROSS2 else 0), (4 if far and p in (GEGLU, FFN) else 2)
                for g in range(lead):
                    body(Step(p, g))
                turns = (GROUPS - tail - lead) // 2
                with eng.Fori(0, turns) as turn:
                    body(Step(p, lead, turn, turns))
                    body(Step(p, lead + 1, turn, turns))
                for g in range(GROUPS - tail, GROUPS):
                    body(Step(p, g))

        def far_stats(s):
            starts = s.turn is None and s.first == GROUPS - 1 and s.phase in (CROSS, CROSS2)
            three = s.ahead(3) if starts or s.phase in (GEGLU, FFN) else None
            return three if three and three.phase in (GEGLU, FFN) else None

        def masked_keys(s, b):
            return (kt[:, b, :, :], kT[s.parity][:, None, b * N:(b + 1) * N].to_broadcast([D, H, N]),
                    headmask[:, :, None].to_broadcast([D, H, N]))

        def halves(ap):
            return ap.rearrange("p (h n) -> p h n", n=N)

        def loads_of(p):
            for key, name in zip("kqv", ("Wk", "Wq", "Wv")):
                k = C if p == CROSS and key != "q" else D
                yield key, raw[p][key][0:k, :], w[f"L0_xattn_{name}{p + 1}"]
            yield "o", raw[p]["o"].rearrange("p (a d) -> p a d", d=D), \
                w[f"L0_xattn_Wo{p + 1}"].rearrange("(a p) d -> p a d", p=128)

        def parts(kind, buf, c, e, k):
            if kind == "fa":
                return buf[0:k, 8 * c:8 * c + 8, :].rearrange("p (q e) d -> p q e d", e=2)[:, :, e, :]
            return buf[0:k, e, 4 * c:4 * c + 4, :]

        def key_copy(s, i):
            bank = stage[cnt.bank("k", s, i)]
            return (kt[:, :, 2 * i:2 * i + 2, :].rearrange("p b h n -> p h b n"),
                    bank[:, :].rearrange("p (h b n) -> p h b n", h=2, b=GB))

        def value_copy(s, i, b):
            t, e, c = i // 4, i // 2 % 2, i % 2
            bank = stage[cnt.bank("z", s, i)]
            return (zt[64 * e:64 * e + 64, 2 * t + b, 4 * c:4 * c + 4, :],
                    bank[64 * b:64 * b + 64, :].rearrange("p (a d) -> p a d", a=4))

        block = ctx.enter_context(nc.Block())

        @block.sync
        def _(sp):
            x = w["x"].rearrange("b n d -> (b n) d").rearrange("(t p) d -> p t d", p=ROWS)

            def load_rows(q):
                n = TILES // 4
                sp.dma_start(rows[:, q * n * D:(q + 1) * n * D].rearrange("p (t d) -> p t d", d=D),
                             x[:, q * n:(q + 1) * n, :]).then_inc(loaded_rows[q > 0], 16)

            def load_vector(dst, name, signal):
                if dst < BIAS:
                    v = w[name].rearrange("(c p) -> p c", p=128)
                    with nc.allow_non_contiguous_dma(reason="vectors of at most 1024 values"):
                        sp.dma_start(cols[:, dst:dst + v.shape[1]], v).then_inc(signal, 16)
                else:
                    sp.dma_start(bias[:, dst - BIAS, :], w[name][None, :].to_broadcast([128, D])).then_inc(signal, 16)

            for key, dst, s in loads_of(SELF):
                sp.dma_start(dst, s).then_inc(loaded_w[SELF][key], 16)
            load_rows(0)
            for dst, name in FIRST_VECTORS.items():
                load_vector(dst, name, loaded_first)
            for key, dst, s in loads_of(CROSS):
                sp.dma_start(dst, s).then_inc(loaded_w[CROSS][key], 16)
            for q in range(1, 4):
                load_rows(q)
            for dst, name in VECTORS.items():
                load_vector(dst, name, loaded_small)
            for dst, s in ((wp[:, :], w["L0_xattn_Wp"]), (w1[:, :], w["L1_xattn_W1"]),
                           (wf[:, :, :], w["L0_xattn_Wf"].rearrange("(a p) d -> p a d", p=128)),
                           (w2[:, :, :], w["L1_xattn_W2"].rearrange("(a p) d -> p a d", p=128)),
                           (wq1[:, :], w["L1_xattn_Wq"]), (wk1[:, :], w["L1_xattn_Wk"]),
                           (wv1[:, :], w["L1_xattn_Wv"]), (wo1[:, :], w["L1_xattn_Wo"])):
                sp.dma_start(dst, s).then_inc(loaded_ffn, 16)
            c = w["ctx_768"].rearrange("b n d -> (b n) d").rearrange("(t p) d -> p t d", p=ROWS)

            def load_ctx(step):
                sp.dma_start(ctx_in[step.parity][:, :, :],
                             c[:, bass.ds(step.at(T), T), :]).then_inc(ctx_loaded[step.parity], 16)

            for p in WITH_CTX:
                for g in range(2):
                    if p == CROSS2:
                        sp.wait_ge(ctx_turned, cnt.at("ctx_turned", Step(CROSS, GROUPS - 2 + g)))
                    load_ctx(Step(p, g))
                with sp.Fori(0, GROUPS // 2 - 1) as turn:
                    for g in range(2):
                        sp.wait_ge(ctx_turned, cnt.at("ctx_turned", Step(p, g, turn, GROUPS // 2 - 1)))
                        load_ctx(Step(p, g + 2, turn, GROUPS // 2 - 1))
            o = out.rearrange("b n d -> (b n) d").rearrange("(t p) d -> p t d", p=ROWS)

            def store(step):
                sp.wait_ge(dve, cnt.at("dve", step, kind="down"))
                sp.dma_start(o[:, bass.ds(step.at(T), T), :],
                             row_slice(rows2, step, 0, T).rearrange("p (t d) -> p t d", d=D)).then_inc(stored, 16)

            with sp.Fori(0, GROUPS // 2 - 1) as turn:
                store(Step(FFN, 0, turn, GROUPS // 2 - 1))
                store(Step(FFN, 1, turn, GROUPS // 2 - 1))
            store(Step(FFN, GROUPS - 2))
            store(Step(FFN, GROUPS - 1))
            sp.wait_ge(stored, 16 * GROUPS)

        @block.tensor
        def _(pe):
            def stage_for(kind, step, i=0):
                n = cnt.uses.index((kind, step.phase, step.first, i))
                return n, stage[n % 3]

            def wait_stage(n, group):
                if group is not None:
                    into = n - cnt.start[("uses", group.phase, group.first)]
                    if into == 2:
                        pe.wait_ge(dve, cnt.start_of("dve", group))
                    if into < 3:
                        return
                elif n < 3:
                    return
                kind, p, g, i = cnt.uses[n - 3]
                turn, turns = (group.turn, group.turns) if group is not None else (None, 1)
                a, v = copiers("up1" if kind == "up" and p == FFN else kind, i)
                if a:
                    pe.wait_ge(act, cnt.at("act", Step(p, g, turn, turns), i, kind=kind))
                if v:
                    pe.wait_ge(dve, cnt.at("dve", Step(p, g, turn, turns), i, kind=kind))

            def three(dst, weights, moving, start=True):
                (wh, wr), (mh, mr) = weights, moving
                nc.tensor.matmul(dst, wh, mh, start=start, stop=False)
                nc.tensor.matmul(dst, wh, mr, start=False, stop=False)
                return nc.tensor.matmul(dst, wr, mh, start=False, stop=True)

            def fold(p):
                s0 = Step(p, 0)
                for m, key in enumerate("kqv"):
                    k = C if p == CROSS and key != "q" else D
                    pe.wait_ge(loaded_w[p][key], 16)
                    for c in range(2):
                        n, bank = stage_for("wt", s0, 2 * m + c)
                        wait_stage(n, None)
                        for q in range(4):
                            last = nc.tensor.transpose(bank[:, q * 128:q * 128 + k],
                                                       raw[p][key][0:k, (4 * c + q) * 128:(4 * c + q + 1) * 128],
                                                       ident[0:k, 0:k])
                        last.then_inc(full, 1)
                pe.wait_ge(act, cnt.at("act", s0, 4, kind="wt"))
                pe.wait_ge(dve, cnt.at("dve", s0, 5, kind="wt"))
                k = kdim[p]
                for i in range(4):
                    c, e = divmod(i, 2)
                    n, bank = stage_for("fa", s0, i)
                    wait_stage(n, None)
                    for q in range(4):
                        last = nc.tensor.matmul(bank[0:k, q * D:(q + 1) * D],
                                                turned_w["k"][64 * e:64 * e + 64, 4 * c + q, 0:k],
                                                turned_w["q"][64 * e:64 * e + 64, 4 * c + q, :], start=True, stop=True)
                    last.then_inc(full, 1)
                pe.wait_ge(loaded_w[p]["o"], 16)
                for i in range(4):
                    c, e = divmod(i, 2)
                    n, bank = stage_for("fb", s0, i)
                    wait_stage(n, None)
                    for q in range(4):
                        last = nc.tensor.matmul(bank[0:k, q * D:(q + 1) * D],
                                                turned_w["v"][64 * e:64 * e + 64, 4 * c + q, 0:k],
                                                raw[p]["o"][64 * e:64 * e + 64, (4 * c + q) * D:(4 * c + q + 1) * D],
                                                start=True, stop=True)
                    last.then_inc(full, 1)

            def x_step(s, group):
                n, bank = stage_for("x", s)
                wait_stage(n, group)
                pe.wait_ge(normed, cnt.at("normed", s))
                if s.phase in WITH_CTX:
                    pe.wait_ge(ctx_loaded[s.parity], cnt.at(f"ctx{s.parity}", s))
                    for t in range(T):
                        last = nc.tensor.transpose(bank[0:C, GR + t * ROWS:GR + (t + 1) * ROWS],
                                                   ctx_in[s.parity][:, t, :], ident[:, :])
                    last.then_inc(ctx_turned, 1)
                for t in range(T):
                    last = nc.tensor.transpose(bank[:, t * ROWS:(t + 1) * ROWS], xn[:, t, :], ident[:, :])
                last.then_inc(full, 1)

            def p_step(s, group, which=range(4)):
                par = s.parity
                if s.phase != CROSS2:
                    pe.wait_ge(rest, cnt.at("rest", s))
                if s.phase in (SELF, CROSS):
                    k = kdim[s.phase]
                    if s.phase == SELF and group is None:
                        pe.wait_ge(act, cnt.at("act", Step(SELF, 0), 3, kind="fb"))
                        pe.wait_ge(dve, cnt.at("dve", Step(SELF, 0), 3, kind="fb"))
                    for i in range(8):
                        n, bank = stage_for("k", s, i)
                        wait_stage(n, group)
                        for e in range(2):
                            last = three(bank[:, e * GR:(e + 1) * GR],
                                         [m[0:k, 2 * i + e, :] for m in fold_a[s.phase]],
                                         [m[0:k, :] for m in src[par]])
                        last.then_inc(full, 1)
                elif s.phase == CROSS2:
                    n, bank = stage_for("qk", s)
                    wait_stage(n, group)
                    nc.tensor.matmul(bank[:, 0:GR], wq1[:, :], xT[par][:, :], start=True, stop=True)
                    nc.tensor.matmul(bank[:, GR:2 * GR], wk1[:, :], cT[par][:, :], start=True, stop=True)\
                        .then_inc(full, 1)
                    n, bank = stage_for("v", s)
                    wait_stage(n, group)
                    for t in range(T):
                        last = nc.tensor.matmul(bank[:, t * D:(t + 1) * D], cT[par][:, t * ROWS:(t + 1) * ROWS],
                                                wv1[:, :], start=True, stop=True)
                    last.then_inc(full, 1)
                else:
                    if s.turn is None and s.first == 0:
                        pe.wait_ge(rest_w, 1 if s.phase == GEGLU else 2)
                    for i in which:
                        n, bank = stage_for("up", s, i)
                        wait_stage(n, group)
                        if s.phase == GEGLU:
                            three(bank[:, 0:GR], [m[:, i * 128:(i + 1) * 128] for m in wp_s], [m[:, :] for m in src[par]])
                            last = three(bank[:, GR:2 * GR], [m[:, FF + i * 128:FF + (i + 1) * 128] for m in wp_s],
                                         [m[:, :] for m in src[par]])
                        else:
                            last = three(bank[:, 0:GR], [m[:, i * 128:(i + 1) * 128] for m in w1_s],
                                         [m[:, :] for m in src[par]])
                        last.then_inc(full, 1)

            def scores_step(s, t, banks=(0, 1)):
                if s.phase == CROSS2 and banks[0] == 0:
                    pe.wait_ge(masked, cnt.at("masked", s, t))
                    if s.turn is None and s.first == 0:
                        pe.wait_ge(masked_dve, t + 1)
                stat = (qT if s.phase == CROSS2 else xT)[s.parity]
                for c in banks:
                    for b in range(2):
                        last = nc.tensor.matmul(scp[64 * b:64 * b + 64, 2 * t + c, :],
                                                stat[:, (2 * t + b) * N:(2 * t + b + 1) * N],
                                                kt[:, 2 * t + b, 8 * c:8 * c + 8, :], start=True, stop=True)
                if banks[-1] == 1:
                    last.then_inc(scores, 1)

            def z_step(s, banks):
                k = kdim[s.phase]
                for i in banks:
                    t, e, c = i // 4, i // 2 % 2, i % 2
                    n, bank = stage_for("z", s, i)
                    wait_stage(n, s)
                    last = three(bank[:, :], [m[0:k, t * ROWS:(t + 1) * ROWS] for m in src[s.parity]],
                                 [m[0:k, e, 4 * c:4 * c + 4, :] for m in fold_b[s.phase]])
                    last.then_inc(full, 1)

            def turn_step(s, t):
                if s.phase == CROSS2:
                    pe.wait_ge(exped, cnt.at("exp", s, t))
                else:
                    pe.wait_ge(probs, cnt.at("probs", s, t))
                for c in range(2):
                    for q in range(4):
                        a = 4 * c + q
                        last = nc.tensor.transpose(scp[:, 2 * t + c, q * 128:(q + 1) * 128],
                                                   pr[t][:, a * 128:(a + 1) * 128], ident[:, :])
                    last.then_inc(turned, 1)

            def out_step(s, t):
                if t == 0:
                    bank, done = out0p, out0
                else:
                    n, bank = stage_for("out1", s)
                    wait_stage(n, s)
                    done = full
                pe.wait_ge(pt_act, cnt.at("pt_act", s, t, 0))
                for a in range(PAIRS):
                    if a == 4:
                        if s.phase == CROSS2:
                            pe.wait_ge(pt_act, cnt.at("pt_act", s, t, 1))
                        else:
                            pe.wait_ge(pt_dve, cnt.at("pt_dve", s, t))
                    if s.phase != CROSS2 and a % 4 == 0:
                        i = 4 * t + 2 + a // 4
                        pe.wait_ge(act, cnt.at("act", s, i, kind="z"))
                        pe.wait_ge(dve, cnt.at("dve", s, i, kind="z"))
                    for b in range(2):
                        if s.phase == CROSS2:
                            v = 2 * (H1 + 1)
                            last = nc.tensor.matmul(bank[64 * b:64 * b + 64, a * v:(a + 1) * v],
                                                    pt[t][:, a, 64 * b:64 * b + 64],
                                                    vb[s.parity][:, 2 * t + b, a, :], start=True, stop=True)
                        else:
                            last = nc.tensor.matmul(bank[64 * b:64 * b + 64, 0:D], pt[t][:, a, 64 * b:64 * b + 64],
                                                    zt[:, 2 * t + b, a, :], start=(a == 0), stop=(a == PAIRS - 1))
                last.then_inc(done, 1)

            def at_step(s, group):
                n, bank = stage_for("at", s)
                wait_stage(n, group)
                pe.wait_ge(dve, cnt.at("dve", s, kind="out1"))
                for t in range(T):
                    last = nc.tensor.transpose(bank[:, t * ROWS:(t + 1) * ROWS], att[:, t, :], ident[:, :])
                last.then_inc(full, 1)

            def wo_step(s, group):
                n, bank = stage_for("wo", s)
                wait_stage(n, group)
                pe.wait_ge(act, cnt.at("act", s, kind="at"))
                for t in range(T):
                    last = nc.tensor.matmul(bank[:, t * D:(t + 1) * D], attT[:, t * ROWS:(t + 1) * ROWS],
                                            wo1[:, :], start=True, stop=True)
                last.then_inc(full, 1)

            def group(s):
                one, two = s.ahead(1), s.ahead(2)
                pe.wait_ge(act, cnt.start_of("act", s))
                pe.wait_ge(dve, cnt.start_of("dve", s) - 1)
                if s.phase in (SELF, CROSS):
                    scores_step(s, 0)
                    scores_step(s, 1)
                    if one.phase != GEGLU:
                        p_step(one, s)
                    z_step(s, (0, 1, 2))
                    turn_step(s, 0)
                    z_step(s, (3,))
                    out_step(s, 0)
                    z_step(s, (4, 5, 6))
                    turn_step(s, 1)
                    z_step(s, (7,))
                    if one.phase == GEGLU:
                        p_step(one, s)
                    x_step(two, s)
                    out_step(s, 1)
                elif s.phase == CROSS2:
                    before, last = s.before(), one.phase != CROSS2
                    if not last:
                        p_step(one, s)
                    scores_step(s, 1)
                    if before:
                        at_step(before, s)
                    turn_step(s, 0)
                    if before:
                        wo_step(before, s)
                    if not last:
                        x_step(two, s)
                    out_step(s, 0)
                    if not last:
                        scores_step(one, 0, (0,))
                    turn_step(s, 1)
                    if not last:
                        scores_step(one, 0, (1,))
                    out_step(s, 1)
                    if last:
                        x_step(two, s)
                        p_step(one, s)
                        at_step(s, s)
                        wo_step(s, s)
                else:
                    if one:
                        p_step(one, s, range(3))
                    if two:
                        x_step(two, s)
                    if one and one.phase == s.phase:
                        p_step(one, s, (3,))
                    n, bank = stage_for("down", s)
                    wait_stage(n, s)
                    wd = wf if s.phase == GEGLU else w2
                    for t in range(T):
                        for i in range(FF // 128):
                            last = nc.tensor.matmul(bank[:, t * D:(t + 1) * D],
                                                    hid[s.parity][:, i, t * ROWS:(t + 1) * ROWS], wd[:, i, :],
                                                    start=(i == 0), stop=(i == FF // 128 - 1))
                    last.then_inc(full, 1)
                    if one and one.phase == CROSS2:
                        scores_step(one, 0)

            pe.wait_ge(made_ident, 2)
            fold(SELF)
            x_step(Step(SELF, 0), None)
            x_step(Step(SELF, 1), None)
            fold(CROSS)
            p_step(Step(SELF, 0), None)
            pe.wait_ge(loaded_ffn, 16 * 8)
            pe.wait_ge(dve, cnt.start[("dve", SELF, 0)])
            each_group(pe, group)

        @block.scalar
        def _(sc):
            def copy(dst, s):
                return nc.scalar.activation(dst, s, ACT.Copy)

            def fold(p):
                s0, k = Step(p, 0), kdim[p]
                for m, key in enumerate("kqv"):
                    kk = k if key != "q" else D
                    sc.wait_ge(full, cnt.at("full", s0, 2 * m, kind="wt"))
                    bank = stage[cnt.bank("wt", s0, 2 * m)]
                    copy(turned_w[key][:, 0:4, 0:kk],
                         bank[:, :].rearrange("p (q k) -> p q k", q=4)[:, :, 0:kk]).then_inc(act, 1)
                for kind, dst in (("fa", fold_a[p]), ("fb", fold_b[p])):
                    for i in range(4):
                        c, e = divmod(i, 2)
                        sc.wait_ge(full, cnt.at("full", s0, i, kind=kind))
                        bank = stage[cnt.bank(kind, s0, i)]
                        copy(parts(kind, dst[0], c, e, k),
                             bank[0:k, :].rearrange("p (q d) -> p q d", q=4)).then_inc(act, 1)

            def x_step(s):
                sc.wait_ge(full, cnt.at("full", s, kind="x"))
                bank = stage[cnt.bank("x", s)]
                if s.phase == CROSS2:
                    last = copy(xT[s.parity][:, :], bank[:, 0:GR])
                else:
                    g = {SELF: G1, CROSS: G2, GEGLU: G3, FFN: G4}[s.phase]
                    last = nc.scalar.activation(xT[s.parity][:, :], bank[:, 0:GR], ACT.Identity,
                                                scale=cols[:, g:g + 1], bias=cols[:, g + 1:g + 2])
                if s.phase in WITH_CTX:
                    last = copy(cT[s.parity][:, :], bank[0:C, GR:2 * GR])
                last.then_inc(act, 1)
                if s.phase == CROSS2:
                    return
                k = C if s.phase == CROSS else D
                sc.wait_ge(act, cnt.at("act", s, kind="x"))
                copy(src[s.parity][0][0:k, :], (cT if s.phase == CROSS else xT)[s.parity][:, :]).then_inc(high, 1)

            def p_step(s, which=range(4)):
                par = s.parity
                if s.phase in (SELF, CROSS):
                    for i in which:
                        if i in K_BY_DVE:
                            continue
                        sc.wait_ge(full, cnt.at("full", s, i, kind="k"))
                        copy(*key_copy(s, i)).then_inc(act, 1)
                elif s.phase == CROSS2:
                    sc.wait_ge(full, cnt.at("full", s, kind="qk"))
                    bank = stage[cnt.bank("qk", s)]
                    nc.scalar.activation(qT[par][:, :], bank[:, 0:GR], ACT.Identity, bias=cols[:, BQ:BQ + 1])
                    nc.scalar.activation(kT[par][:, :], bank[:, GR:2 * GR], ACT.Identity,
                                         bias=cols[:, BK:BK + 1]).then_inc(act, 1)
                else:
                    for i in which:
                        sc.wait_ge(full, cnt.at("full", s, i, kind="up"))
                        bank = stage[cnt.bank("up", s, i)]
                        if s.phase == GEGLU:
                            if i >= 2:
                                sc.wait_ge(dve, cnt.at("dve", s, i - 2, kind="up"))
                            nc.scalar.activation(ge[i % 2][:, :], bank[:, GR:2 * GR], ACT.Gelu,
                                                 bias=cols[:, BP + 4 + i:BP + 5 + i]).then_inc(gelued, 1)
                        else:
                            nc.scalar.activation(hid[par][:, i, :], bank[:, 0:GR], ACT.Gelu,
                                                 bias=cols[:, BF1 + i:BF1 + i + 1]).then_inc(act, 1)

            def exp_step(s, t):
                sc.wait_ge(shifted, cnt.at("shifted", s, t))
                nc.scalar.activation(pr[t][:, :], pr[t][:, :], ACT.Exp, scale=scale[s.phase]).then_inc(exped, 1)

            def load_table(function):
                nc.scalar.activation(seen_act[:, :], ident[:, 0:1], function)

            def pt_step(s, t):
                banks = 2 if s.phase == CROSS2 else 1
                for c in range(banks):
                    sc.wait_ge(turned, cnt.at("turned", s, t, c))
                    copy(pt[t][:, 4 * c:4 * c + 4, :],
                         scp[:, 2 * t + c, :].rearrange("p (q n) -> p q n", q=4)).then_inc(pt_act, 1)

            def z_step(s, banks):
                for i in banks:
                    sc.wait_ge(full, cnt.at("full", s, i, kind="z"))
                    for b in range(2 if i in Z_BY_ACT else 1):
                        copy(*value_copy(s, i, b)).then_inc(act, 1)

            def at_step(s):
                sc.wait_ge(full, cnt.at("full", s, kind="at"))
                copy(attT[:, :], stage[cnt.bank("at", s)][:, 0:GR]).then_inc(act, 1)

            def group(s):
                one, two = s.ahead(1), s.ahead(2)
                if s.phase in (SELF, CROSS):
                    if one.phase == GEGLU:
                        exp_step(s, 0)
                        z_step(s, (0,))
                        exp_step(s, 1)
                        z_step(s, (1, 2))
                        load_table(ACT.Gelu)
                    else:
                        p_step(one, range(2))
                        exp_step(s, 0)
                        p_step(one, range(2, 5))
                        exp_step(s, 1)
                        p_step(one, range(5, 8))
                        z_step(s, (0, 1, 2))
                    pt_step(s, 0)
                    z_step(s, (3, 4, 5, 6))
                    pt_step(s, 1)
                    z_step(s, (7,))
                    if one.phase == GEGLU:
                        p_step(one)
                    x_step(two)
                elif s.phase == CROSS2:
                    before, last = s.before(), one.phase != CROSS2
                    if not last:
                        p_step(one)
                    exp_step(s, 0)
                    if before:
                        at_step(before)
                    pt_step(s, 0)
                    if not last:
                        x_step(two)
                    exp_step(s, 1)
                    pt_step(s, 1)
                    if last:
                        load_table(ACT.Gelu)
                        x_step(two)
                        p_step(one)
                        at_step(s)
                else:
                    if one:
                        p_step(one, range(3))
                    if two:
                        x_step(two)
                    if one and one.phase == s.phase:
                        p_step(one, (3,))
                    if one and one.phase == CROSS2:
                        load_table(ACT.Exp)

            sc.wait_ge(made_ident, 2)
            load_table(ACT.Exp)
            fold(SELF)
            sc.wait_ge(loaded_first, 16 * len(FIRST_VECTORS))
            x_step(Step(SELF, 0))
            x_step(Step(SELF, 1))
            fold(CROSS)
            p_step(Step(SELF, 0), range(8))
            sc.wait_ge(loaded_ffn, 16 * 8)
            copy(wp_s[0][:, :], wp[:, :]).then_inc(high_w, 1)
            copy(w1_s[0][:, :], w1[:, :]).then_inc(high_w, 1)
            sc.wait_ge(loaded_small, 16 * len(VECTORS))
            each_group(sc, group)

        @block.vector
        def _(ve):
            def fold_turn(p):
                s0, k = Step(p, 0), kdim[p]
                for m, key in enumerate("kqv"):
                    kk = k if key != "q" else D
                    ve.wait_ge(full, cnt.at("full", s0, 2 * m + 1, kind="wt"))
                    bank = stage[cnt.bank("wt", s0, 2 * m + 1)]
                    nc.vector.tensor_copy(turned_w[key][:, 4:8, 0:kk],
                                          bank[:, :].rearrange("p (q k) -> p q k", q=4)[:, :, 0:kk]).then_inc(dve, 1)

            def fold_rest(p, kind, dst):
                s0, k = Step(p, 0), kdim[p]
                for i in range(4):
                    c, e = divmod(i, 2)
                    ve.wait_ge(act, cnt.at("act", s0, i, kind=kind))
                    bank = stage[cnt.bank(kind, s0, i)]
                    nc.vector.tensor_tensor(parts(kind, dst[1], c, e, k),
                                            bank[0:k, :].rearrange("p (q d) -> p q d", q=4),
                                            parts(kind, dst[0].bitcast(F32), c, e, k), ALU.subtract).then_inc(dve, 1)

            def stats_step(s):
                buf = rows2 if s.phase == FFN else rows
                for t in range(T):
                    last = nc.vector.bn_stats(stats[s.parity][:, t, :], row_slice(buf, s, t))
                last.then_inc(stated, 1)
                ve.wait_ge(stated, cnt.at("stats", s))
                nc.vector.tensor_copy(seen[:, :], stats[s.parity][:, T - 1, 0:1])
                for t in range(T):
                    last = nc.vector.bn_aggr(mv[s.parity][:, t, :], stats[s.parity][:, t, :])
                last.then_inc(meaned, 1)
                ve.wait_ge(meaned, cnt.at("mean", s))
                nc.vector.tensor_scalar(veps[s.parity][:, :], mv[s.parity][:, :, 1], EPS, None, ALU.add)\
                    .then_inc(epsed, 1)

            def norm_step(s):
                if s.phase == CROSS2:
                    nc.vector.tensor_copy(xn[:, :, :], row_slice(rows, s, 0, T).rearrange("p (t d) -> p t d", t=T))\
                        .then_inc(normed, 1)
                    return
                ve.wait_ge(rooted, cnt.at("rstd", s))
                buf = rows2 if s.phase == FFN else rows
                for t in range(T):
                    last = nc.vector.tensor_scalar(xn[:, t, :], row_slice(buf, s, t), mv[s.parity][:, t, 0:1],
                                                   rstd[s.parity][:, t:t + 1], ALU.subtract, ALU.mult)
                last.then_inc(normed, 1)

            def p_step(s, which=range(4)):
                par = s.parity
                if s.phase in (SELF, CROSS):
                    for i in K_BY_DVE:
                        ve.wait_ge(full, cnt.at("full", s, i, kind="k"))
                        nc.vector.tensor_copy(*key_copy(s, i)).then_inc(dve, 1)
                elif s.phase == CROSS2 and which[0] == 0:
                    ve.wait_ge(full, cnt.at("full", s, kind="v"))
                    bank = stage[cnt.bank("v", s)]
                    for t in range(T):
                        for b in range(2):
                            for e in range(2):
                                h = slice(64 * b, 64 * b + 64)
                                v = bank[h, t * D:(t + 1) * D].rearrange("p (a e d) -> p a e d", e=2, d=H1)[:, :, e, :]
                                vv = bias[h, BV, :].rearrange("p (a e d) -> p a e d", e=2, d=H1)[:, :, e, :]
                                last = nc.vector.tensor_tensor(
                                    vb[par][64 * e:64 * e + 64, 2 * t + b, :, e * (H1 + 1):e * (H1 + 1) + H1],
                                    v, vv, ALU.add)
                    last.then_inc(dve, 1)
                elif s.phase == GEGLU:
                    for i in which:
                        ve.wait_ge(gelued, cnt.at("gelu", s, i))
                        bank = stage[cnt.bank("up", s, i)]
                        nc.vector.scalar_tensor_tensor(hid[par][:, i, :], bank[:, 0:GR], cols[:, BP + i:BP + i + 1],
                                                       ge[i % 2][:, :], op0=ALU.add, op1=ALU.mult).then_inc(dve, 1)

            def max_step(s, t):
                ve.wait_ge(scores, cnt.at("scores", s, t))
                sc3 = scp[:, 2 * t:2 * t + 2, :].rearrange("p c (h n) -> p (c h) n", n=N)
                nc.vector.tensor_reduce(mx[:, t, :], sc3, AX.X, ALU.max).then_inc(maxed, 1)
                ve.wait_ge(maxed, cnt.at("max", s, t))
                nc.vector.tensor_tensor(halves(pr[t][:, :]), sc3, mx[:, t, :, None].to_broadcast([ROWS, H, N]),
                                        ALU.subtract).then_inc(shifted, 1)

            def sum_step(s, t):
                ve.wait_ge(exped, cnt.at("exp", s, t))
                nc.vector.tensor_reduce(sm[:, t, :], halves(pr[t][:, :]), AX.X, ALU.add).then_inc(summed, 1)
                ve.wait_ge(summed, cnt.at("sums", s, t))
                nc.vector.reciprocal(rc[:, t, :], sm[:, t, :]).then_inc(recip, 1)

            def z_step(s, banks):
                for i in banks:
                    if i not in Z_BY_ACT:
                        ve.wait_ge(full, cnt.at("full", s, i, kind="z"))
                        nc.vector.tensor_copy(*value_copy(s, i, 1)).then_inc(dve, 1)

            def pt_step(s, t):
                ve.wait_ge(turned, cnt.at("turned", s, t, 1))
                nc.vector.tensor_copy(pt[t][:, 4:8, :],
                                      scp[:, 2 * t + 1, :].rearrange("p (q n) -> p q n", q=4)).then_inc(pt_dve, 1)

            def out_step(s, t):
                if t == 0:
                    ve.wait_ge(out0, cnt.at("out0", s))
                    bank = out0p
                else:
                    ve.wait_ge(full, cnt.at("full", s, kind="out1"))
                    bank = stage[cnt.bank("out1", s)]
                if s.phase == CROSS2:
                    o = bank[:, 0:H * (H1 + 1)].rearrange("p (h v) -> p h v", v=H1 + 1)
                    nc.vector.reciprocal(rc[:, t, :, None], o[:, :, H1:H1 + 1]).then_inc(normr, 1)
                    ve.wait_ge(normr, cnt.at("norm", s, t))
                    last = nc.vector.tensor_tensor(att[:, t, :].rearrange("p (h v) -> p h v", v=H1), o[:, :, 0:H1],
                                                   rc[:, t, :, None].to_broadcast([ROWS, H, H1]), ALU.mult)
                    if t == 1:
                        last.then_inc(dve, 1)
                else:
                    r = row_slice(rows, s, t)
                    last = nc.vector.tensor_tensor(r, bank[:, 0:D], r, ALU.add)
                    if t == 1:
                        last.then_inc(dve, 1)

            def wo_step(s):
                ve.wait_ge(full, cnt.at("full", s, kind="wo"))
                bank = stage[cnt.bank("wo", s)]
                nc.vector.tensor_tensor(row_slice(rows2, s, 0, T).rearrange("p (t d) -> p t d", t=T),
                                        bank[:, 0:GR].rearrange("p (t d) -> p t d", t=T),
                                        bias[:, None, BO3, :].to_broadcast([ROWS, T, D]), ALU.add).then_inc(dve, 1)

            def group(s):
                one, two = s.ahead(1), s.ahead(2)
                three = far_stats(s)
                if s.phase in (SELF, CROSS):
                    stats_step(two)
                    max_step(s, 0)
                    max_step(s, 1)
                    sum_step(s, 0)
                    if one.phase != GEGLU:
                        p_step(one)
                    sum_step(s, 1)
                    norm_step(two)
                    z_step(s, (0, 1, 2))
                    pt_step(s, 0)
                    z_step(s, (3, 4))
                    out_step(s, 0)
                    z_step(s, (5, 6))
                    pt_step(s, 1)
                    z_step(s, (7,))
                    if one.phase == GEGLU:
                        p_step(one)
                        stats_step(three)
                    out_step(s, 1)
                elif s.phase == CROSS2:
                    before, last = s.before(), one.phase != CROSS2
                    max_step(s, 0)
                    if before:
                        out_step(before, 1)
                    if last:
                        max_step(s, 1)
                    if two.phase == FFN:
                        stats_step(two)
                    norm_step(two)
                    if not last:
                        p_step(one)
                        max_step(s, 1)
                    if before:
                        wo_step(before)
                    out_step(s, 0)
                    if last:
                        stats_step(three)
                        out_step(s, 1)
                        wo_step(s)
                else:
                    if two:
                        norm_step(two)
                    if s.phase == GEGLU:
                        p_step(one)
                    if one and one.phase == CROSS2:
                        ve.wait_ge(act, cnt.at("act", one, kind="qk"))
                        for t in range(T):
                            nc.vector.tensor_tensor(*masked_keys(one, 2 * t + 1), ALU.mult).then_inc(masked_dve, 1)
                    if three:
                        stats_step(three)
                    ve.wait_ge(full, cnt.at("full", s, kind="down"))
                    if s.phase == GEGLU:
                        ve.wait_ge(biased, cnt.at("biased", s))
                    else:
                        ve.wait_ge(summed2, cnt.at("summed2", s))
                    bank = stage[cnt.bank("down", s)]
                    r = row_slice(rows if s.phase == GEGLU else rows2, s, 0, T)
                    nc.vector.tensor_tensor(r, bank[:, 0:GR], r, ALU.add).then_inc(dve, 1)

            fold_turn(SELF)
            ve.wait_ge(loaded_rows[0], 16)
            stats_step(Step(SELF, 0))
            stats_step(Step(SELF, 1))
            fold_rest(SELF, "fa", fold_a[SELF])
            norm_step(Step(SELF, 0))
            fold_rest(SELF, "fb", fold_b[SELF])
            ve.wait_ge(full, cnt.at("full", Step(SELF, 0), kind="x"))
            norm_step(Step(SELF, 1))
            fold_turn(CROSS)
            fold_rest(CROSS, "fa", fold_a[CROSS])
            fold_rest(CROSS, "fb", fold_b[CROSS])
            p_step(Step(SELF, 0))
            ve.wait_ge(loaded_rows[1], 48)
            ve.wait_ge(loaded_small, 16 * len(VECTORS))
            each_group(ve, group, far=True)

        @block.gpsimd
        def _(gp):
            nc.gpsimd.memset(ident[:, :], 0.0).then_inc(made_ident, 1)
            gp.wait_ge(made_ident, 1)
            nc.gpsimd.affine_select(out=ident[:, :], in_=ident[:, :], compare_op=ALU.not_equal, fill=1.0, base=0,
                                    pattern=[[-1, 128]], channel_multiplier=1).then_inc(made_ident, 1)
            nc.gpsimd.memset(neghalf[:, :], -0.5).then_inc(made_half, 1)
            nc.gpsimd.memset(headmask[:, :], 1.0).then_inc(made_mask, 1)
            gp.wait_ge(made_mask, 1)
            nc.gpsimd.affine_select(out=headmask[:, :], in_=headmask[:, :], compare_op=ALU.is_ge, fill=0.0, base=0,
                                    pattern=[[-H1, H]], channel_multiplier=1).then_inc(made_mask, 1)
            gp.wait_ge(made_mask, 2)
            nc.gpsimd.affine_select(out=headmask[:, :], in_=headmask[:, :], compare_op=ALU.is_ge, fill=0.0, base=H1 - 1,
                                    pattern=[[H1, H]], channel_multiplier=-1).then_inc(made_mask, 1)
            for n in range(2):
                nc.gpsimd.memset(vb[n][:, :, :, :], 0.0).then_inc(made_vb, 1)
            gp.wait_ge(made_vb, 2)
            for n in range(2):
                for e in range(2):
                    one = (e + 1) * (H1 + 1) - 1
                    nc.gpsimd.memset(vb[n][64 * e:64 * e + 64, :, :, one:one + 1], 1.0).then_inc(made_vb, 1)

            def rstd_step(s):
                gp.wait_ge(epsed, cnt.at("rstd", s))
                nc.gpsimd.tensor_tensor(rstd[s.parity][:, :], veps[s.parity][:, :], neghalf[:, :], ALU.pow)\
                    .then_inc(rooted, 1)

            def bias_step(s):
                if s.phase == CROSS2:
                    return
                gp.wait_ge(normed, cnt.at("normed", s))
                buf = rows2 if s.phase == FFN else rows
                r = row_slice(buf, s, 0, T)
                r3 = r.rearrange("p (t d) -> p t d", t=T)
                b = {SELF: BO1, CROSS: BO2, GEGLU: BFF, FFN: BLAST}[s.phase]
                nc.gpsimd.tensor_tensor(r3, r3, bias[:, None, b, :].to_broadcast([ROWS, T, D]), ALU.add)\
                    .then_inc(biased, 1)
                if s.phase == FFN:
                    gp.wait_ge(biased, cnt.at("biased", s))
                    nc.gpsimd.tensor_tensor(r, r, row_slice(rows, s, 0, T), ALU.add).then_inc(summed2, 1)

            def rest_step(s):
                if s.phase == CROSS2:
                    return
                k = C if s.phase == CROSS else D
                gp.wait_ge(high, cnt.at("high", s))
                hp, rp = src[s.parity]
                nc.gpsimd.tensor_tensor(rp[0:k, :], (cT if s.phase == CROSS else xT)[s.parity][:, :],
                                        hp.bitcast(F32)[0:k, :], ALU.subtract).then_inc(rest, 1)

            def mask_step(s, group):
                gp.wait_ge(act, cnt.at("act", s, kind="qk"))
                for t in range(T):
                    if group.phase == CROSS2:
                        gp.wait_ge(scores, cnt.at("scores", group, t))
                    for b in (2 * t, 2 * t + 1) if group.phase == CROSS2 else (2 * t,):
                        last = nc.gpsimd.tensor_tensor(*masked_keys(s, b), ALU.mult)
                    last.then_inc(masked, 1)

            def group(s):
                one, two = s.ahead(1), s.ahead(2)
                three = far_stats(s)
                if s.phase in (SELF, CROSS) or (s.phase == CROSS2 and two.phase == FFN):
                    rstd_step(two)
                if s.phase in (SELF, CROSS):
                    for t in range(T):
                        gp.wait_ge(recip, cnt.at("recip", s, t))
                        nc.gpsimd.tensor_tensor(halves(pr[t][:, :]), halves(pr[t][:, :]),
                                                rc[:, t, :, None].to_broadcast([ROWS, H, N]), ALU.mult).then_inc(probs, 1)
                    bias_step(two)
                    rest_step(two)
                    if three:
                        rstd_step(three)
                else:
                    if one and one.phase == CROSS2:
                        mask_step(one, s)
                    if two:
                        rest_step(two)
                    if three:
                        rstd_step(three)
                    if two:
                        bias_step(two)

            gp.wait_ge(loaded_first, 16 * len(FIRST_VECTORS))
            gp.wait_ge(made_half, 1)
            gp.wait_ge(made_mask, 3)
            gp.wait_ge(made_vb, 6)
            for g in range(2):
                rstd_step(Step(SELF, g))
            for g in range(2):
                bias_step(Step(SELF, g))
                rest_step(Step(SELF, g))
            for n, (whole, s) in enumerate(((wp, wp_s), (w1, w1_s))):
                gp.wait_ge(high_w, n + 1)
                nc.gpsimd.tensor_tensor(s[1][:, :], whole[:, :], s[0].bitcast(F32)[:, :], ALU.subtract).then_inc(rest_w, 1)
            gp.wait_ge(loaded_small, 16 * len(VECTORS))
            each_group(gp, group, far=True)


_OUTS = [((B, N, D), "float32")]


def kernel(**inputs):
    import numpy as _np
    import concourse.bacc as _bacc
    from concourse import mybir as _mybir
    from concourse.bass_utils import run_bass_kernel_spmd as _run

    nc = _bacc.Bacc("TRN2", target_bir_lowering=False, num_devices=1)
    arrays, aps = {}, {}
    for name, value in inputs.items():
        a = _np.ascontiguousarray(value)
        arrays[f"in_{name}_dram"] = a
        aps[name] = nc.dram_tensor(f"in_{name}_dram", a.shape, _mybir.dt.from_np(a.dtype), kind="ExternalInput").ap()
    outs = [nc.dram_tensor(f"out_{i}_dram", shape, _mybir.dt.from_np(_np.dtype(dtype)), kind="ExternalOutput").ap()
            for i, (shape, dtype) in enumerate(_OUTS)]
    attention_blocks(nc, aps, outs[0])
    r = _run(nc, [arrays], core_ids=[0])
    return r.results[0]["out_0_dram"]
```

```python
import concourse.bass as bass
from concourse import mybir
from contextlib import ExitStack

F32 = mybir.dt.float32
F32R = mybir.dt.float32r
ACT = mybir.ActivationFunctionType
ALU = mybir.AluOpType
AX = mybir.AxisListType

B, N, D, C = 32, 64, 128, 96
H, DH = 16, 64
H1 = D // H
FF = 4 * D
EPS = 1e-5
ROWS = 128
TILES = B * N // ROWS
T = 2
GB = T * ROWS // N
GR = T * ROWS
GROUPS = TILES // T
PAIRS = H // 2
BANK = 512
SELF, CROSS, GEGLU, CROSS2, FFN = range(5)
PHASES = 5
WARM_UP = 12
WITH_CTX = (CROSS, CROSS2)

K_BY_DVE = (3, 6)
Z_BY_ACT = (0,)


def copiers(kind, i):
    if kind in ("fa", "fb"):
        return 1, 1
    if kind == "wt":
        return (1, 0) if i % 2 == 0 else (0, 1)
    if kind == "k":
        return (0, 1) if i in K_BY_DVE else (1, 0)
    if kind == "z":
        return (2, 0) if i in Z_BY_ACT else (1, 1)
    if kind in ("x", "qk", "at", "up1"):
        return 1, 0
    return 0, 1


class Step:

    def __init__(self, phase, first, turn=None, turns=1):
        self.phase, self.first, self.turn, self.turns = phase, first, turn, turns
        self.parity = first % 2

    def ahead(self, k):
        if self.first + k < GROUPS:
            return Step(self.phase, self.first + k, self.turn, self.turns)
        assert self.turn is None
        return Step(self.phase + 1, self.first + k - GROUPS) if self.phase + 1 < PHASES else None

    def before(self):
        return Step(self.phase, self.first - 1, self.turn, self.turns) if self.first > 0 else None

    def at(self, scale, offset=0):
        if self.turn is None:
            return self.first * scale + offset
        return self.turn * (2 * scale) + (self.first * scale + offset)


class Counts:

    def __init__(self):
        self.total, self.value, self.uses, self.start = {}, {}, [], {}
        self.fold_turn(SELF)
        self.fold_product(SELF)
        self.x(SELF, 0)
        self.fold_turn(CROSS)
        self.x(SELF, 1)
        self.fold_product(CROSS)
        self.p(SELF, 0)
        for p in range(PHASES):
            for g in range(GROUPS):
                self.group(p, g)

    def tick(self, name, key, n=1):
        self.total[name] = self.total.get(name, 0) + n
        self.value[(name, *key)] = self.total[name]

    def use(self, kind, p, g, i=0):
        self.tick("full", (kind, p, g, i))
        for name, n in zip(("act", "dve"), copiers("up1" if kind == "up" and p == FFN else kind, i)):
            self.tick(name, (kind, p, g, i), n)
        self.uses.append((kind, p, g, i))

    def fold_turn(self, p):
        for i in range(6):
            self.use("wt", p, 0, i)

    def fold_product(self, p):
        for kind in ("fa", "fb"):
            for i in range(4):
                self.use(kind, p, 0, i)

    def x(self, p, g):
        if p != CROSS2:
            for name in ("stats", "mean", "rstd", "biased"):
                self.tick(name, (p, g))
            if p == FFN:
                self.tick("summed2", (p, g))
        self.tick("normed", (p, g))
        if p != CROSS2:
            self.tick("high", (p, g))
            self.tick("rest", (p, g))
        if p in WITH_CTX:
            self.tick(f"ctx{g % 2}", (p, g), 16)
            self.tick("ctx_turned", (p, g))
        self.use("x", p, g)

    def p(self, p, g, which=range(4)):
        for kind, n in {SELF: [("k", 8)], CROSS: [("k", 8)], CROSS2: [("qk", 1), ("v", 1)]}.get(p, [("up", 4)]):
            for i in which if kind == "up" else range(n):
                self.use(kind, p, g, i)
                if kind == "up" and p == GEGLU:
                    self.tick("gelu", (p, g, i))
        if p == CROSS2:
            for t in range(T):
                self.tick("masked", (p, g, t))

    def group(self, p, g):
        self.start[("act", p, g)] = self.total["act"]
        self.start[("dve", p, g)] = self.total["dve"]
        self.start[("uses", p, g)] = len(self.uses)
        one, two = Step(p, g).ahead(1), Step(p, g).ahead(2)
        if p in (SELF, CROSS):
            for t in range(T):
                self.softmax(p, g, t)
            if one.phase != GEGLU:
                self.p(one.phase, one.first)
            for t in range(T):
                for i in range(3):
                    self.use("z", p, g, 4 * t + i)
                if one.phase == GEGLU and t == 0:
                    self.p(one.phase, one.first, (0, 1))
                self.turned(p, g, t)
                self.use("z", p, g, 4 * t + 3)
                if t == 0:
                    self.tick("out0", (p, g))
            if one.phase == GEGLU:
                self.p(one.phase, one.first, (2, 3))
            self.x(two.phase, two.first)
            self.use("out1", p, g)
        elif p == CROSS2:
            if one.phase == CROSS2:
                self.p(one.phase, one.first)
            self.softmax(p, g, 1)
            if g > 0:
                self.finish(p, g - 1)
            self.turned(p, g, 0)
            if one.phase == CROSS2:
                self.x(two.phase, two.first)
            self.tick("out0", (p, g))
            if one.phase != CROSS2:
                self.p(one.phase, one.first, (0, 1))
            self.turned(p, g, 1)
            if one.phase == CROSS2:
                self.softmax(one.phase, one.first, 0)
            self.use("out1", p, g)
            for t in range(T):
                self.tick("norm", (p, g, t))
            if one.phase != CROSS2:
                self.x(two.phase, two.first)
                self.use("at", p, g)
                self.p(one.phase, one.first, (2, 3))
                self.use("wo", p, g)
        else:
            if one:
                self.p(one.phase, one.first, (0, 1))
            if two:
                self.x(two.phase, two.first)
            if one and one.phase == p:
                self.p(one.phase, one.first, (2, 3))
            self.use("down", p, g)
            if one and one.phase == CROSS2:
                self.softmax(one.phase, one.first, 0)

    def softmax(self, p, g, t):
        for name in ("scores", "max", "shifted", "exp"):
            self.tick(name, (p, g, t))
        if p != CROSS2:
            for name in ("sums", "recip", "probs"):
                self.tick(name, (p, g, t))

    def turned(self, p, g, t):
        for c in range(2):
            self.tick("turned", (p, g, t, c))
        if p == CROSS2:
            for c in range(2):
                self.tick("pt_act", (p, g, t, c))
        else:
            self.tick("pt_act", (p, g, t, 0))
            self.tick("pt_dve", (p, g, t))

    def finish(self, p, g):
        self.use("at", p, g)
        self.use("wo", p, g)

    def linear(self, of, step):
        v = of(step.first)
        if step.turn is None:
            return v
        per = of(step.first + 2) - v
        for n in range(1, step.turns):
            assert of(step.first + 2 * n) == v + n * per, step
        return step.turn * per + v

    def at(self, name, step, *rest, kind=None):
        head = (name,) if kind is None else (name, kind)
        tail = rest if kind is None else (rest or (0,))
        return self.linear(lambda g: self.value[(*head, step.phase, g, *tail)], step)

    def start_of(self, name, step):
        return self.linear(lambda g: self.start[(name, step.phase, g)], step)

    def bank(self, kind, step, i=0):
        return self.uses.index((kind, step.phase, step.first, i)) % 3


def attention_blocks(nc, w, out):
    cnt = Counts()
    ctx = ExitStack()
    with ctx:
        def sb(name, shape, dt=F32):
            return ctx.enter_context(nc.sbuf_tensor(name, shape, dt))

        def ps(name, shape):
            return ctx.enter_context(nc.psum_tensor(name, shape, F32))

        def sem(name):
            return ctx.enter_context(nc.semaphore(name))

        rows = sb("rows", [ROWS, TILES * D])
        rows2 = sb("rows2", [ROWS, TILES * D])
        ident = sb("ident", [128, 128])
        headmask = sb("headmask", [128, H])
        fold_a = [[sb(f"fold_a{p}{n}", [128, H, D], F32R) for n in "hr"] for p in (SELF, CROSS)]
        fold_b = [[sb(f"fold_b{p}{n}", [128, 2, PAIRS, D], F32R) for n in "hr"] for p in (SELF, CROSS)]
        wp = sb("wp", [D, 2 * FF])
        wp_s = [sb(f"wp_{n}", [D, 2 * FF], F32R) for n in "hr"]
        w1 = sb("w1", [D, FF])
        w1_s = [sb(f"w1_{n}", [D, FF], F32R) for n in "hr"]
        wf = sb("wf", [128, FF // 128, D])
        w2 = sb("w2", [128, FF // 128, D])
        wq1, wo1 = sb("wq1", [D, D]), sb("wo1", [D, D])
        wk1, wv1 = sb("wk1", [C, D]), sb("wv1", [C, D])
        cols = sb("cols", [128, 22])
        bias = sb("bias", [128, 6, D])
        neghalf = sb("neghalf", [128, T])
        seen, seen_act = sb("seen", [ROWS, 1]), sb("seen_act", [ROWS, 1])
        ctx_in = [sb(f"ctx_in{n}", [ROWS, T, C]) for n in range(2)]
        stats = [sb(f"stats{n}", [128, T, 6]) for n in range(2)]
        mv = [sb(f"mv{n}", [128, T, 2]) for n in range(2)]
        veps = [sb(f"veps{n}", [128, T]) for n in range(2)]
        rstd = [sb(f"rstd{n}", [128, T]) for n in range(2)]
        xn = sb("xn", [ROWS, T, D])
        xT = [sb(f"xT{n}", [D, GR]) for n in range(2)]
        cT = [sb(f"cT{n}", [C, GR]) for n in range(2)]
        src = [[sb(f"src{n}{m}", [D, GR], F32R) for m in "hr"] for n in range(2)]
        kt = sb("kt", [D, GB, H, N])
        zt = sb("zt", [128, GB, PAIRS, D])
        pr = [sb(f"pr{t}", [ROWS, H * N]) for t in range(T)]
        mx = sb("mx", [ROWS, T, H])
        sm = sb("sm", [ROWS, T, H])
        rc = sb("rc", [ROWS, T, H])
        pt = [sb(f"pt{t}", [128, PAIRS, ROWS]) for t in range(T)]
        raw = {SELF: {k: zt[:, n, :, :].rearrange("p a d -> p (a d)") for n, k in enumerate("kqvo")},
               CROSS: dict(zip("kqvo", (pr[0][:, :], pr[1][:, :], *(b[:, :, :].rearrange("p a n -> p (a n)") for b in pt))))}
        turned_w = {k: kt[:, n, :, :].rearrange("p h n -> p (h n)").rearrange("p (a k) -> p a k", k=128)
                    for n, k in enumerate("kqv")}
        ge = [sb(f"ge{n}", [128, GR]) for n in range(2)]
        hid = [sb(f"hid{n}", [128, FF // 128, GR]) for n in range(2)]
        qT, kT = ([sb(f"{m}T{n}", [D, GR]) for n in range(2)] for m in "qk")
        vb = [sb(f"vb{n}", [128, GB, PAIRS, 2 * (H1 + 1)]) for n in range(2)]
        att = sb("att", [ROWS, T, D])
        attT = sb("attT", [D, GR])

        G1, B1_, G2, B2_, G3, B3_, G4, B4_ = range(8)
        BQ, BK, BP, BF1 = 8, 9, 10, 18
        BO1, BO2, BFF, BO3, BV, BLAST = range(6)
        BIAS = 100
        FIRST_VECTORS = {G1: "L0_xattn_g1", B1_: "L0_xattn_b1", BIAS + BO1: "L0_xattn_bo1"}
        VECTORS = {G2: "L0_xattn_g2", B2_: "L0_xattn_b2", G3: "L0_xattn_g3", B3_: "L0_xattn_b3", G4: "L1_xattn_ln_g",
                   B4_: "L1_xattn_ln_b", BQ: "L1_xattn_bq", BK: "L1_xattn_bk", BP: "L0_xattn_bp", BF1: "L1_xattn_b1",
                   BIAS + BO2: "L0_xattn_bo2", BIAS + BFF: "L0_xattn_bf", BIAS + BO3: "L1_xattn_bo",
                   BIAS + BV: "L1_xattn_bv", BIAS + BLAST: "L1_xattn_b2"}

        scp = ps("scp", [128, 4, BANK])
        stage = [ps(f"stage{n}", [128, BANK]) for n in range(3)]
        out0p = ps("out0p", [128, BANK])

        full = sem("stage_full")
        act = sem("stage_copied_act")
        dve = sem("stage_copied_dve")
        scores = sem("scores")
        maxed = sem("maxed")
        shifted = sem("shifted")
        exped = sem("exped")
        summed = sem("summed")
        recip = sem("recip")
        probs = sem("probs")
        turned = sem("turned")
        pt_act = sem("pt_act")
        pt_dve = sem("pt_dve")
        out0 = sem("out0")
        stated = sem("stated")
        meaned = sem("meaned")
        epsed = sem("epsed")
        rooted = sem("rooted")
        normed = sem("normed")
        biased = sem("biased")
        summed2 = sem("summed2")
        high = sem("high")
        rest = sem("rest")
        ctx_loaded = [sem("ctx_loaded0"), sem("ctx_loaded1")]
        ctx_turned = sem("ctx_turned")
        gelued = sem("gelued")
        masked = sem("masked")
        masked_dve = sem("masked_dve")
        normr = sem("normr")
        loaded_rows = [sem("loaded_rows0"), sem("loaded_rows1")]
        loaded_w = [{k: sem(f"loaded_w{k}{p}") for k in "kqvo"} for p in (SELF, CROSS)]
        loaded_first = sem("loaded_first")
        loaded_small = sem("loaded_small")
        loaded_ffn = sem("loaded_ffn")
        made_ident = sem("made_ident")
        made_mask = sem("made_mask")
        made_half = sem("made_half")
        made_vb = sem("made_vb")
        high_w = sem("high_w")
        rest_w = sem("rest_w")
        stored = sem("stored")

        scale = {SELF: DH ** -0.5, CROSS: DH ** -0.5, CROSS2: H1 ** -0.5}
        kdim = {SELF: D, CROSS: C}

        def row_slice(buf, step, t=0, n=1):
            return buf[:, bass.ds(step.at(T * D, t * D), n * D)]

        def each_group(eng, body, looks_far=False):
            for p in range(PHASES):
                lead, tail = (2 if p == CROSS2 else 0), (4 if looks_far and p in (GEGLU, FFN) else 2)
                for g in range(lead):
                    body(Step(p, g))
                turns = (GROUPS - tail - lead) // 2
                with eng.Fori(0, turns) as turn:
                    body(Step(p, lead, turn, turns))
                    body(Step(p, lead + 1, turn, turns))
                for g in range(GROUPS - tail, GROUPS):
                    body(Step(p, g))

        def own_bank(kind, step):
            return kind == "down" or (kind == "up" and step.first >= 1) or \
                (kind == "x" and (step.first < 2 if step.phase == CROSS2 else step.first >= 2 and step.phase in (GEGLU, FFN)))

        def home(kind, step, i=0):
            if not own_bank(kind, step):
                return stage[cnt.bank(kind, step, i)]
            if kind == "down":
                return scp[:, 2 + step.parity, :]
            if kind == "x":
                return scp[:, 1, :]
            end = (cnt.start[("uses", step.phase, 0)] - 1) % 3
            return (stage[(end + 1) % 3], stage[(end + 2) % 3], out0p, stage[end])[i]

        def far(s):
            starts = s.turn is None and s.first == GROUPS - 1 and s.phase in (CROSS, CROSS2)
            three = s.ahead(3) if starts or s.phase in (GEGLU, FFN) else None
            return three if three and three.phase in (GEGLU, FFN) else None

        def masked_keys(s, b):
            return (kt[:, b, :, :], kT[s.parity][:, None, b * N:(b + 1) * N].to_broadcast([D, H, N]),
                    headmask[:, :, None].to_broadcast([D, H, N]))

        def halves(ap):
            return ap.rearrange("p (h n) -> p h n", n=N)

        def loads_of(p):
            for key, name in zip("kqv", ("Wk", "Wq", "Wv")):
                k = C if p == CROSS and key != "q" else D
                yield key, raw[p][key][0:k, :], w[f"L0_xattn_{name}{p + 1}"]
            yield "o", raw[p]["o"].rearrange("p (a d) -> p a d", d=D), \
                w[f"L0_xattn_Wo{p + 1}"].rearrange("(a p) d -> p a d", p=128)

        def parts(kind, buf, c, e, k):
            if kind == "fa":
                return buf[0:k, 8 * c:8 * c + 8, :].rearrange("p (q e) d -> p q e d", e=2)[:, :, e, :]
            return buf[0:k, e, 4 * c:4 * c + 4, :]

        def key_copy(s, i):
            bank = home("k", s, i)
            return (kt[:, :, 2 * i:2 * i + 2, :].rearrange("p b h n -> p h b n"),
                    bank[:, :].rearrange("p (h b n) -> p h b n", h=2, b=GB))

        def value_copy(s, i, b):
            t, e, c = i // 4, i // 2 % 2, i % 2
            bank = home("z", s, i)
            return (zt[64 * e:64 * e + 64, 2 * t + b, 4 * c:4 * c + 4, :],
                    bank[64 * b:64 * b + 64, :].rearrange("p (a d) -> p a d", a=4))

        block = ctx.enter_context(nc.Block())

        @block.sync
        def _(sp):
            x = w["x"].rearrange("b n d -> (b n) d").rearrange("(t p) d -> p t d", p=ROWS)

            def load_rows(q):
                n = TILES // 4
                sp.dma_start(rows[:, q * n * D:(q + 1) * n * D].rearrange("p (t d) -> p t d", d=D),
                             x[:, q * n:(q + 1) * n, :]).then_inc(loaded_rows[q > 0], 16)

            def load_vector(dst, name, signal):
                if dst < BIAS:
                    v = w[name].rearrange("(c p) -> p c", p=128)
                    with nc.allow_non_contiguous_dma(reason="vectors of at most 1024 values"):
                        sp.dma_start(cols[:, dst:dst + v.shape[1]], v).then_inc(signal, 16)
                else:
                    sp.dma_start(bias[:, dst - BIAS, :], w[name][None, :].to_broadcast([128, D])).then_inc(signal, 16)

            for key, dst, s in loads_of(SELF):
                sp.dma_start(dst, s).then_inc(loaded_w[SELF][key], 16)
                if key == "k":
                    load_rows(0)
            for dst, name in FIRST_VECTORS.items():
                load_vector(dst, name, loaded_first)
            for key, dst, s in loads_of(CROSS):
                sp.dma_start(dst, s).then_inc(loaded_w[CROSS][key], 16)
            for q in range(1, 4):
                load_rows(q)
            for dst, name in VECTORS.items():
                load_vector(dst, name, loaded_small)
            for dst, s in ((wp[:, :], w["L0_xattn_Wp"]), (w1[:, :], w["L1_xattn_W1"]),
                           (wf[:, :, :], w["L0_xattn_Wf"].rearrange("(a p) d -> p a d", p=128)),
                           (w2[:, :, :], w["L1_xattn_W2"].rearrange("(a p) d -> p a d", p=128)),
                           (wq1[:, :], w["L1_xattn_Wq"]), (wk1[:, :], w["L1_xattn_Wk"]),
                           (wv1[:, :], w["L1_xattn_Wv"]), (wo1[:, :], w["L1_xattn_Wo"])):
                sp.dma_start(dst, s).then_inc(loaded_ffn, 16)
            c = w["ctx_768"].rearrange("b n d -> (b n) d").rearrange("(t p) d -> p t d", p=ROWS)

            def load_ctx(step):
                sp.dma_start(ctx_in[step.parity][:, :, :],
                             c[:, bass.ds(step.at(T), T), :]).then_inc(ctx_loaded[step.parity], 16)

            for p in WITH_CTX:
                for g in range(2):
                    if p == CROSS2:
                        sp.wait_ge(ctx_turned, cnt.at("ctx_turned", Step(CROSS, GROUPS - 2 + g)))
                    load_ctx(Step(p, g))
                with sp.Fori(0, GROUPS // 2 - 1) as turn:
                    for g in range(2):
                        sp.wait_ge(ctx_turned, cnt.at("ctx_turned", Step(p, g, turn, GROUPS // 2 - 1)))
                        load_ctx(Step(p, g + 2, turn, GROUPS // 2 - 1))
            o = out.rearrange("b n d -> (b n) d").rearrange("(t p) d -> p t d", p=ROWS)

            def store(step):
                sp.wait_ge(dve, cnt.at("dve", step, kind="down"))
                sp.dma_start(o[:, bass.ds(step.at(T), T), :],
                             row_slice(rows2, step, 0, T).rearrange("p (t d) -> p t d", d=D)).then_inc(stored, 16)

            with sp.Fori(0, GROUPS // 2 - 1) as turn:
                store(Step(FFN, 0, turn, GROUPS // 2 - 1))
                store(Step(FFN, 1, turn, GROUPS // 2 - 1))
            store(Step(FFN, GROUPS - 2))
            store(Step(FFN, GROUPS - 1))
            sp.wait_ge(stored, 16 * GROUPS)

        @block.tensor
        def _(pe):
            def stage_for(group, kind, step, i=0):
                n = cnt.uses.index((kind, step.phase, step.first, i))
                bank = home(kind, step, i)
                if own_bank(kind, step):
                    if kind == "up" and i == 3:
                        pe.wait_ge(dve, cnt.start_of("dve", group))
                    return bank
                if group is not None:
                    into = n - cnt.start[("uses", group.phase, group.first)]
                    if into == 2 and cnt.uses[n - 3][0] != "down":
                        pe.wait_ge(dve, cnt.start_of("dve", group))
                    if into < 3:
                        return bank
                elif n < 3:
                    return bank
                kind, p, g, i = cnt.uses[n - 3]
                turn, turns = (group.turn, group.turns) if group is not None else (None, 1)
                a, v = copiers("up1" if kind == "up" and p == FFN else kind, i)
                if a:
                    pe.wait_ge(act, cnt.at("act", Step(p, g, turn, turns), i, kind=kind))
                if v:
                    pe.wait_ge(dve, cnt.at("dve", Step(p, g, turn, turns), i, kind=kind))
                return bank

            def three(dst, weights, moving, start=True):
                (wh, wr), (mh, mr) = weights, moving
                nc.tensor.matmul(dst, wh, mh, start=start, stop=False)
                nc.tensor.matmul(dst, wh, mr, start=False, stop=False)
                return nc.tensor.matmul(dst, wr, mh, start=False, stop=True)

            def fold_turn(p):
                s0 = Step(p, 0)
                for m, key in enumerate("kqv"):
                    k = C if p == CROSS and key != "q" else D
                    pe.wait_ge(loaded_w[p][key], 16)
                    for c in range(2):
                        bank = stage_for(None, "wt", s0, 2 * m + c)
                        for q in range(4):
                            last = nc.tensor.transpose(bank[:, q * 128:q * 128 + k],
                                                       raw[p][key][0:k, (4 * c + q) * 128:(4 * c + q + 1) * 128],
                                                       ident[0:k, 0:k])
                        last.then_inc(full, 1)

            def fold_product(p):
                s0, k = Step(p, 0), kdim[p]
                pe.wait_ge(act, cnt.at("act", s0, 2, kind="wt"))
                pe.wait_ge(dve, cnt.at("dve", s0, 3, kind="wt"))
                for i in range(4):
                    c, e = divmod(i, 2)
                    bank = stage_for(None, "fa", s0, i)
                    for q in range(4):
                        last = nc.tensor.matmul(bank[0:k, q * D:(q + 1) * D],
                                                turned_w["k"][64 * e:64 * e + 64, 4 * c + q, 0:k],
                                                turned_w["q"][64 * e:64 * e + 64, 4 * c + q, :], start=True, stop=True)
                    last.then_inc(full, 1)
                pe.wait_ge(act, cnt.at("act", s0, 4, kind="wt"))
                pe.wait_ge(dve, cnt.at("dve", s0, 5, kind="wt"))
                pe.wait_ge(loaded_w[p]["o"], 16)
                for i in range(4):
                    c, e = divmod(i, 2)
                    bank = stage_for(None, "fb", s0, i)
                    for q in range(4):
                        last = nc.tensor.matmul(bank[0:k, q * D:(q + 1) * D],
                                                turned_w["v"][64 * e:64 * e + 64, 4 * c + q, 0:k],
                                                raw[p]["o"][64 * e:64 * e + 64, (4 * c + q) * D:(4 * c + q + 1) * D],
                                                start=True, stop=True)
                    last.then_inc(full, 1)

            def x_step(s, group):
                bank = stage_for(group, "x", s)
                pe.wait_ge(normed, cnt.at("normed", s))
                if s.phase in WITH_CTX:
                    pe.wait_ge(ctx_loaded[s.parity], cnt.at(f"ctx{s.parity}", s))
                    for t in range(T):
                        last = nc.tensor.transpose(bank[0:C, GR + t * ROWS:GR + (t + 1) * ROWS],
                                                   ctx_in[s.parity][:, t, :], ident[:, :])
                    last.then_inc(ctx_turned, 1)
                for t in range(T):
                    last = nc.tensor.transpose(bank[:, t * ROWS:(t + 1) * ROWS], xn[:, t, :], ident[:, :])
                last.then_inc(full, 1)

            def p_step(s, group, which=range(4)):
                par = s.parity
                if s.phase != CROSS2 and which[0] == 0:
                    pe.wait_ge(rest, cnt.at("rest", s))
                if s.phase in (SELF, CROSS):
                    k = kdim[s.phase]
                    if s.phase == SELF and group is None:
                        pe.wait_ge(act, cnt.at("act", Step(SELF, 0), 3, kind="fb"))
                        pe.wait_ge(dve, cnt.at("dve", Step(SELF, 0), 3, kind="fb"))
                    for i in range(8):
                        bank = stage_for(group, "k", s, i)
                        for e in range(2):
                            last = three(bank[:, e * GR:(e + 1) * GR],
                                         [m[0:k, 2 * i + e, :] for m in fold_a[s.phase]],
                                         [m[0:k, :] for m in src[par]])
                        last.then_inc(full, 1)
                elif s.phase == CROSS2:
                    bank = stage_for(group, "qk", s)
                    nc.tensor.matmul(bank[:, 0:GR], wq1[:, :], xT[par][:, :], start=True, stop=True)
                    nc.tensor.matmul(bank[:, GR:2 * GR], wk1[:, :], cT[par][:, :], start=True, stop=True)\
                        .then_inc(full, 1)
                    bank = stage_for(group, "v", s)
                    for t in range(T):
                        last = nc.tensor.matmul(bank[:, t * D:(t + 1) * D], cT[par][:, t * ROWS:(t + 1) * ROWS],
                                                wv1[:, :], start=True, stop=True)
                    last.then_inc(full, 1)
                else:
                    if s.turn is None and s.first == 0 and which[0] == 0:
                        pe.wait_ge(rest_w, 1 if s.phase == GEGLU else 2)
                    for i in which:
                        bank = stage_for(group, "up", s, i)
                        if s.phase == GEGLU:
                            three(bank[:, 0:GR], [m[:, i * 128:(i + 1) * 128] for m in wp_s], [m[:, :] for m in src[par]])
                            last = three(bank[:, GR:2 * GR], [m[:, FF + i * 128:FF + (i + 1) * 128] for m in wp_s],
                                         [m[:, :] for m in src[par]])
                        else:
                            last = three(bank[:, 0:GR], [m[:, i * 128:(i + 1) * 128] for m in w1_s],
                                         [m[:, :] for m in src[par]])
                        last.then_inc(full, 1)

            def scores_step(s, t, banks=(0, 1)):
                if s.phase == CROSS2 and s.turn is None and s.first == 0 and banks[0] == 0:
                    if t == 0:
                        pe.wait_ge(act, cnt.at("act", Step(CROSS2, 1), kind="x"))
                    else:
                        pe.wait_ge(dve, cnt.at("dve", Step(GEGLU, GROUPS - 1), kind="down"))
                if s.phase == CROSS2 and banks[0] == 0:
                    pe.wait_ge(masked, cnt.at("masked", s, t))
                    if s.turn is None and s.first == 0:
                        pe.wait_ge(masked_dve, t + 1)
                stat = (qT if s.phase == CROSS2 else xT)[s.parity]
                for c in banks:
                    for b in range(2):
                        last = nc.tensor.matmul(scp[64 * b:64 * b + 64, 2 * t + c, :],
                                                stat[:, (2 * t + b) * N:(2 * t + b + 1) * N],
                                                kt[:, 2 * t + b, 8 * c:8 * c + 8, :], start=True, stop=True)
                if banks[-1] == 1:
                    last.then_inc(scores, 1)

            def z_step(s, banks):
                k = kdim[s.phase]
                for i in banks:
                    t, e, c = i // 4, i // 2 % 2, i % 2
                    bank = stage_for(s, "z", s, i)
                    last = three(bank[:, :], [m[0:k, t * ROWS:(t + 1) * ROWS] for m in src[s.parity]],
                                 [m[0:k, e, 4 * c:4 * c + 4, :] for m in fold_b[s.phase]])
                    last.then_inc(full, 1)

            def turn_step(s, t):
                if s.phase == CROSS2:
                    pe.wait_ge(exped, cnt.at("exp", s, t))
                else:
                    pe.wait_ge(probs, cnt.at("probs", s, t))
                for c in range(2):
                    for q in range(4):
                        a = 4 * c + q
                        last = nc.tensor.transpose(scp[:, 2 * t + c, q * 128:(q + 1) * 128],
                                                   pr[t][:, a * 128:(a + 1) * 128], ident[:, :])
                    last.then_inc(turned, 1)

            def out_step(s, t):
                if t == 0:
                    bank, done = out0p, out0
                else:
                    bank = stage_for(s, "out1", s)
                    done = full
                pe.wait_ge(pt_act, cnt.at("pt_act", s, t, 0))
                for a in range(PAIRS):
                    if a == 4:
                        if s.phase == CROSS2:
                            pe.wait_ge(pt_act, cnt.at("pt_act", s, t, 1))
                        else:
                            pe.wait_ge(pt_dve, cnt.at("pt_dve", s, t))
                    if s.phase != CROSS2 and a % 4 == 0:
                        i = 4 * t + 2 + a // 4
                        pe.wait_ge(act, cnt.at("act", s, i, kind="z"))
                        pe.wait_ge(dve, cnt.at("dve", s, i, kind="z"))
                    for b in range(2):
                        if s.phase == CROSS2:
                            v = 2 * (H1 + 1)
                            last = nc.tensor.matmul(bank[64 * b:64 * b + 64, a * v:(a + 1) * v],
                                                    pt[t][:, a, 64 * b:64 * b + 64],
                                                    vb[s.parity][:, 2 * t + b, a, :], start=True, stop=True)
                        else:
                            last = nc.tensor.matmul(bank[64 * b:64 * b + 64, 0:D], pt[t][:, a, 64 * b:64 * b + 64],
                                                    zt[:, 2 * t + b, a, :], start=(a == 0), stop=(a == PAIRS - 1))
                last.then_inc(done, 1)

            def at_step(s, group):
                bank = stage_for(group, "at", s)
                pe.wait_ge(dve, cnt.at("dve", s, kind="out1"))
                for t in range(T):
                    last = nc.tensor.transpose(bank[:, t * ROWS:(t + 1) * ROWS], att[:, t, :], ident[:, :])
                last.then_inc(full, 1)

            def wo_step(s, group):
                bank = stage_for(group, "wo", s)
                pe.wait_ge(act, cnt.at("act", s, kind="at"))
                for t in range(T):
                    last = nc.tensor.matmul(bank[:, t * D:(t + 1) * D], attT[:, t * ROWS:(t + 1) * ROWS],
                                            wo1[:, :], start=True, stop=True)
                last.then_inc(full, 1)

            def group(s):
                one, two = s.ahead(1), s.ahead(2)
                pe.wait_ge(act, cnt.start_of("act", s))
                pe.wait_ge(dve, cnt.start_of("dve", s) - 1)
                if s.phase in (SELF, CROSS):
                    scores_step(s, 0)
                    scores_step(s, 1)
                    if one.phase != GEGLU:
                        p_step(one, s)
                    z_step(s, (0, 1, 2))
                    if one.phase == GEGLU:
                        p_step(one, s, (0, 1))
                    turn_step(s, 0)
                    z_step(s, (3,))
                    out_step(s, 0)
                    z_step(s, (4, 5, 6))
                    turn_step(s, 1)
                    z_step(s, (7,))
                    if one.phase == GEGLU:
                        p_step(one, s, (2, 3))
                    x_step(two, s)
                    out_step(s, 1)
                elif s.phase == CROSS2:
                    before, last = s.before(), one.phase != CROSS2
                    if not last:
                        p_step(one, s)
                    scores_step(s, 1)
                    if before:
                        at_step(before, s)
                    turn_step(s, 0)
                    if before:
                        wo_step(before, s)
                    if not last:
                        x_step(two, s)
                    out_step(s, 0)
                    if last:
                        p_step(one, s, (0,))
                    else:
                        scores_step(one, 0, (0,))
                    turn_step(s, 1)
                    if last:
                        p_step(one, s, (1,))
                    else:
                        scores_step(one, 0, (1,))
                    out_step(s, 1)
                    if last:
                        x_step(two, s)
                        at_step(s, s)
                        p_step(one, s, (2, 3))
                        wo_step(s, s)
                else:
                    if one:
                        p_step(one, s, (0, 1))
                    if two:
                        x_step(two, s)
                    if one and one.phase == s.phase:
                        p_step(one, s, (2, 3))
                    bank = home("down", s)
                    wd = wf if s.phase == GEGLU else w2
                    for t in range(T):
                        for i in range(FF // 128):
                            last = nc.tensor.matmul(bank[:, t * D:(t + 1) * D],
                                                    hid[s.parity][:, i, t * ROWS:(t + 1) * ROWS], wd[:, i, :],
                                                    start=(i == 0), stop=(i == FF // 128 - 1))
                    last.then_inc(full, 1)
                    if one and one.phase == CROSS2:
                        scores_step(one, 0)

            pe.wait_ge(made_ident, 2)
            for _ in range(WARM_UP):
                nc.tensor.transpose(scp[:, 0, 0:128], ident[:, :], ident[:, :])
            fold_turn(SELF)
            fold_product(SELF)
            x_step(Step(SELF, 0), None)
            fold_turn(CROSS)
            x_step(Step(SELF, 1), None)
            fold_product(CROSS)
            p_step(Step(SELF, 0), None)
            pe.wait_ge(loaded_ffn, 16 * 8)
            pe.wait_ge(dve, cnt.start[("dve", SELF, 0)])
            each_group(pe, group)

        @block.scalar
        def _(sc):
            def copy(dst, s):
                return nc.scalar.activation(dst, s, ACT.Copy)

            def fold_turn(p):
                s0, k = Step(p, 0), kdim[p]
                for m, key in enumerate("kqv"):
                    kk = k if key != "q" else D
                    sc.wait_ge(full, cnt.at("full", s0, 2 * m, kind="wt"))
                    bank = home("wt", s0, 2 * m)
                    copy(turned_w[key][:, 0:4, 0:kk],
                         bank[:, :].rearrange("p (q k) -> p q k", q=4)[:, :, 0:kk]).then_inc(act, 1)

            def fold_high(p):
                s0, k = Step(p, 0), kdim[p]
                for kind, dst in (("fa", fold_a[p]), ("fb", fold_b[p])):
                    for i in range(4):
                        c, e = divmod(i, 2)
                        sc.wait_ge(full, cnt.at("full", s0, i, kind=kind))
                        bank = home(kind, s0, i)
                        copy(parts(kind, dst[0], c, e, k),
                             bank[0:k, :].rearrange("p (q d) -> p q d", q=4)).then_inc(act, 1)

            def x_step(s):
                sc.wait_ge(full, cnt.at("full", s, kind="x"))
                bank = home("x", s)
                if s.phase == CROSS2:
                    last = copy(xT[s.parity][:, :], bank[:, 0:GR])
                else:
                    g = {SELF: G1, CROSS: G2, GEGLU: G3, FFN: G4}[s.phase]
                    last = nc.scalar.activation(xT[s.parity][:, :], bank[:, 0:GR], ACT.Identity,
                                                scale=cols[:, g:g + 1], bias=cols[:, g + 1:g + 2])
                if s.phase in WITH_CTX:
                    last = copy(cT[s.parity][:, :], bank[0:C, GR:2 * GR])
                last.then_inc(act, 1)
                if s.phase == CROSS2:
                    return
                k = C if s.phase == CROSS else D
                sc.wait_ge(act, cnt.at("act", s, kind="x"))
                copy(src[s.parity][0][0:k, :], (cT if s.phase == CROSS else xT)[s.parity][:, :]).then_inc(high, 1)

            def p_step(s, which=range(4)):
                par = s.parity
                if s.phase in (SELF, CROSS):
                    for i in which:
                        if i in K_BY_DVE:
                            continue
                        sc.wait_ge(full, cnt.at("full", s, i, kind="k"))
                        copy(*key_copy(s, i)).then_inc(act, 1)
                elif s.phase == CROSS2:
                    sc.wait_ge(full, cnt.at("full", s, kind="qk"))
                    bank = home("qk", s)
                    nc.scalar.activation(qT[par][:, :], bank[:, 0:GR], ACT.Identity, bias=cols[:, BQ:BQ + 1])
                    nc.scalar.activation(kT[par][:, :], bank[:, GR:2 * GR], ACT.Identity,
                                         bias=cols[:, BK:BK + 1]).then_inc(act, 1)
                else:
                    for i in which:
                        sc.wait_ge(full, cnt.at("full", s, i, kind="up"))
                        bank = home("up", s, i)
                        if s.phase == GEGLU:
                            if i >= 2:
                                sc.wait_ge(dve, cnt.at("dve", s, i - 2, kind="up"))
                            nc.scalar.activation(ge[i % 2][:, :], bank[:, GR:2 * GR], ACT.Gelu,
                                                 bias=cols[:, BP + 4 + i:BP + 5 + i]).then_inc(gelued, 1)
                        else:
                            nc.scalar.activation(hid[par][:, i, :], bank[:, 0:GR], ACT.Gelu,
                                                 bias=cols[:, BF1 + i:BF1 + i + 1]).then_inc(act, 1)

            def exp_step(s, t):
                sc.wait_ge(shifted, cnt.at("shifted", s, t))
                nc.scalar.activation(pr[t][:, :], pr[t][:, :], ACT.Exp, scale=scale[s.phase]).then_inc(exped, 1)

            def load_table(function):
                nc.scalar.activation(seen_act[:, :], ident[:, 0:1], function)

            def pt_step(s, t):
                banks = 2 if s.phase == CROSS2 else 1
                for c in range(banks):
                    sc.wait_ge(turned, cnt.at("turned", s, t, c))
                    copy(pt[t][:, 4 * c:4 * c + 4, :],
                         scp[:, 2 * t + c, :].rearrange("p (q n) -> p q n", q=4)).then_inc(pt_act, 1)

            def z_step(s, banks):
                for i in banks:
                    sc.wait_ge(full, cnt.at("full", s, i, kind="z"))
                    for b in range(2 if i in Z_BY_ACT else 1):
                        copy(*value_copy(s, i, b)).then_inc(act, 1)

            def at_step(s):
                sc.wait_ge(full, cnt.at("full", s, kind="at"))
                copy(attT[:, :], home("at", s)[:, 0:GR]).then_inc(act, 1)

            def group(s):
                one, two = s.ahead(1), s.ahead(2)
                if s.phase in (SELF, CROSS):
                    if one.phase == GEGLU:
                        exp_step(s, 0)
                        z_step(s, (0,))
                        exp_step(s, 1)
                        z_step(s, (1, 2))
                        load_table(ACT.Gelu)
                        p_step(one, (0, 1))
                    else:
                        p_step(one, range(3))
                        exp_step(s, 0)
                        p_step(one, range(3, 6))
                        exp_step(s, 1)
                        p_step(one, range(6, 8))
                        z_step(s, (0, 1, 2))
                    pt_step(s, 0)
                    z_step(s, (3, 4, 5, 6))
                    pt_step(s, 1)
                    z_step(s, (7,))
                    if one.phase == GEGLU:
                        p_step(one, (2, 3))
                    x_step(two)
                elif s.phase == CROSS2:
                    before, last = s.before(), one.phase != CROSS2
                    if not last:
                        p_step(one)
                    exp_step(s, 0)
                    if before:
                        at_step(before)
                    pt_step(s, 0)
                    if not last:
                        x_step(two)
                    exp_step(s, 1)
                    pt_step(s, 1)
                    if last:
                        load_table(ACT.Gelu)
                        p_step(one, (0, 1))
                        x_step(two)
                        at_step(s)
                        p_step(one, (2, 3))
                else:
                    if one:
                        p_step(one, (0, 1))
                    if two:
                        x_step(two)
                    if one and one.phase == s.phase:
                        p_step(one, (2, 3))
                    if one and one.phase == CROSS2:
                        load_table(ACT.Exp)

            sc.wait_ge(made_ident, 2)
            load_table(ACT.Exp)
            fold_turn(SELF)
            fold_high(SELF)
            sc.wait_ge(loaded_first, 16 * len(FIRST_VECTORS))
            x_step(Step(SELF, 0))
            fold_turn(CROSS)
            x_step(Step(SELF, 1))
            fold_high(CROSS)
            p_step(Step(SELF, 0), range(8))
            sc.wait_ge(loaded_ffn, 16 * 8)
            copy(wp_s[0][:, :], wp[:, :]).then_inc(high_w, 1)
            copy(w1_s[0][:, :], w1[:, :]).then_inc(high_w, 1)
            sc.wait_ge(loaded_small, 16 * len(VECTORS))
            each_group(sc, group)

        @block.vector
        def _(ve):
            def fold_turn(p):
                s0, k = Step(p, 0), kdim[p]
                for m, key in enumerate("kqv"):
                    kk = k if key != "q" else D
                    ve.wait_ge(full, cnt.at("full", s0, 2 * m + 1, kind="wt"))
                    bank = home("wt", s0, 2 * m + 1)
                    nc.vector.tensor_copy(turned_w[key][:, 4:8, 0:kk],
                                          bank[:, :].rearrange("p (q k) -> p q k", q=4)[:, :, 0:kk]).then_inc(dve, 1)

            def fold_rest(p, kind, dst):
                s0, k = Step(p, 0), kdim[p]
                for i in range(4):
                    c, e = divmod(i, 2)
                    ve.wait_ge(act, cnt.at("act", s0, i, kind=kind))
                    bank = home(kind, s0, i)
                    nc.vector.tensor_tensor(parts(kind, dst[1], c, e, k),
                                            bank[0:k, :].rearrange("p (q d) -> p q d", q=4),
                                            parts(kind, dst[0].bitcast(F32), c, e, k), ALU.subtract).then_inc(dve, 1)

            def stats_step(s):
                buf = rows2 if s.phase == FFN else rows
                for t in range(T):
                    last = nc.vector.bn_stats(stats[s.parity][:, t, :], row_slice(buf, s, t))
                last.then_inc(stated, 1)
                ve.wait_ge(stated, cnt.at("stats", s))
                nc.vector.tensor_copy(seen[:, :], stats[s.parity][:, T - 1, 0:1])
                for t in range(T):
                    last = nc.vector.bn_aggr(mv[s.parity][:, t, :], stats[s.parity][:, t, :])
                last.then_inc(meaned, 1)
                ve.wait_ge(meaned, cnt.at("mean", s))
                nc.vector.tensor_scalar(veps[s.parity][:, :], mv[s.parity][:, :, 1], EPS, None, ALU.add)\
                    .then_inc(epsed, 1)

            def norm_step(s, turned=None):
                if turned:
                    ve.wait_ge(full, cnt.at("full", turned, kind="x"))
                if s.phase == CROSS2:
                    nc.vector.tensor_copy(xn[:, :, :], row_slice(rows, s, 0, T).rearrange("p (t d) -> p t d", t=T))\
                        .then_inc(normed, 1)
                    return
                ve.wait_ge(rooted, cnt.at("rstd", s))
                buf = rows2 if s.phase == FFN else rows
                for t in range(T):
                    last = nc.vector.tensor_scalar(xn[:, t, :], row_slice(buf, s, t), mv[s.parity][:, t, 0:1],
                                                   rstd[s.parity][:, t:t + 1], ALU.subtract, ALU.mult)
                last.then_inc(normed, 1)

            def p_step(s, which=range(4)):
                par = s.parity
                if s.phase in (SELF, CROSS):
                    for i in which:
                        if i not in K_BY_DVE:
                            continue
                        ve.wait_ge(full, cnt.at("full", s, i, kind="k"))
                        nc.vector.tensor_copy(*key_copy(s, i)).then_inc(dve, 1)
                elif s.phase == CROSS2 and which[0] == 0:
                    ve.wait_ge(full, cnt.at("full", s, kind="v"))
                    bank = home("v", s)
                    for t in range(T):
                        for b in range(2):
                            for e in range(2):
                                h = slice(64 * b, 64 * b + 64)
                                v = bank[h, t * D:(t + 1) * D].rearrange("p (a e d) -> p a e d", e=2, d=H1)[:, :, e, :]
                                vv = bias[h, BV, :].rearrange("p (a e d) -> p a e d", e=2, d=H1)[:, :, e, :]
                                last = nc.vector.tensor_tensor(
                                    vb[par][64 * e:64 * e + 64, 2 * t + b, :, e * (H1 + 1):e * (H1 + 1) + H1],
                                    v, vv, ALU.add)
                    last.then_inc(dve, 1)
                elif s.phase == GEGLU:
                    for i in which:
                        ve.wait_ge(gelued, cnt.at("gelu", s, i))
                        bank = home("up", s, i)
                        nc.vector.scalar_tensor_tensor(hid[par][:, i, :], bank[:, 0:GR], cols[:, BP + i:BP + i + 1],
                                                       ge[i % 2][:, :], op0=ALU.add, op1=ALU.mult).then_inc(dve, 1)

            def max_step(s, t):
                ve.wait_ge(scores, cnt.at("scores", s, t))
                sc3 = scp[:, 2 * t:2 * t + 2, :].rearrange("p c (h n) -> p (c h) n", n=N)
                nc.vector.tensor_reduce(mx[:, t, :], sc3, AX.X, ALU.max).then_inc(maxed, 1)

            def shift_step(s, t):
                sc3 = scp[:, 2 * t:2 * t + 2, :].rearrange("p c (h n) -> p (c h) n", n=N)
                ve.wait_ge(maxed, cnt.at("max", s, t))
                nc.vector.tensor_tensor(halves(pr[t][:, :]), sc3, mx[:, t, :, None].to_broadcast([ROWS, H, N]),
                                        ALU.subtract).then_inc(shifted, 1)

            def sum_step(s, t):
                ve.wait_ge(exped, cnt.at("exp", s, t))
                nc.vector.tensor_reduce(sm[:, t, :], halves(pr[t][:, :]), AX.X, ALU.add).then_inc(summed, 1)
                ve.wait_ge(summed, cnt.at("sums", s, t))
                nc.vector.reciprocal(rc[:, t, :], sm[:, t, :]).then_inc(recip, 1)

            def z_step(s, banks):
                for i in banks:
                    if i not in Z_BY_ACT:
                        ve.wait_ge(full, cnt.at("full", s, i, kind="z"))
                        nc.vector.tensor_copy(*value_copy(s, i, 1)).then_inc(dve, 1)

            def pt_step(s, t):
                ve.wait_ge(turned, cnt.at("turned", s, t, 1))
                nc.vector.tensor_copy(pt[t][:, 4:8, :],
                                      scp[:, 2 * t + 1, :].rearrange("p (q n) -> p q n", q=4)).then_inc(pt_dve, 1)

            def out_step(s, t):
                if t == 0:
                    ve.wait_ge(out0, cnt.at("out0", s))
                    bank = out0p
                else:
                    ve.wait_ge(full, cnt.at("full", s, kind="out1"))
                    bank = home("out1", s)
                if s.phase == CROSS2:
                    o = bank[:, 0:H * (H1 + 1)].rearrange("p (h v) -> p h v", v=H1 + 1)
                    nc.vector.reciprocal(rc[:, t, :, None], o[:, :, H1:H1 + 1]).then_inc(normr, 1)
                    ve.wait_ge(normr, cnt.at("norm", s, t))
                    last = nc.vector.tensor_tensor(att[:, t, :].rearrange("p (h v) -> p h v", v=H1), o[:, :, 0:H1],
                                                   rc[:, t, :, None].to_broadcast([ROWS, H, H1]), ALU.mult)
                    if t == 1:
                        last.then_inc(dve, 1)
                else:
                    r = row_slice(rows, s, t)
                    last = nc.vector.tensor_tensor(r, bank[:, 0:D], r, ALU.add)
                    if t == 1:
                        last.then_inc(dve, 1)

            def wo_step(s):
                ve.wait_ge(full, cnt.at("full", s, kind="wo"))
                bank = home("wo", s)
                nc.vector.tensor_tensor(row_slice(rows2, s, 0, T).rearrange("p (t d) -> p t d", t=T),
                                        bank[:, 0:GR].rearrange("p (t d) -> p t d", t=T),
                                        bias[:, None, BO3, :].to_broadcast([ROWS, T, D]), ALU.add).then_inc(dve, 1)

            def group(s):
                one, two = s.ahead(1), s.ahead(2)
                three = far(s)
                if s.phase in (SELF, CROSS):
                    stats_step(two)
                    max_step(s, 0)
                    shift_step(s, 0)
                    max_step(s, 1)
                    shift_step(s, 1)
                    if one.phase != GEGLU:
                        p_step(one, range(4))
                    sum_step(s, 0)
                    if one.phase != GEGLU:
                        p_step(one, range(4, 8))
                    else:
                        z_step(s, (0, 1, 2))
                    sum_step(s, 1)
                    if one.phase == GEGLU:
                        p_step(one, (0, 1))
                    else:
                        z_step(s, (0, 1, 2))
                    pt_step(s, 0)
                    z_step(s, (3,))
                    norm_step(two)
                    z_step(s, (4,))
                    out_step(s, 0)
                    z_step(s, (5, 6))
                    pt_step(s, 1)
                    z_step(s, (7,))
                    if one.phase == GEGLU:
                        p_step(one, (2, 3))
                        stats_step(three)
                    out_step(s, 1)
                    if three:
                        norm_step(three, two)
                elif s.phase == CROSS2:
                    before, last = s.before(), one.phase != CROSS2
                    max_step(s, 0)
                    shift_step(s, 0)
                    if before:
                        out_step(before, 1)
                    if last:
                        max_step(s, 1)
                        shift_step(s, 1)
                    if two.phase == FFN:
                        stats_step(two)
                    norm_step(two)
                    if not last:
                        p_step(one)
                        max_step(s, 1)
                        shift_step(s, 1)
                    if before:
                        wo_step(before)
                    out_step(s, 0)
                    if last:
                        stats_step(three)
                        out_step(s, 1)
                        wo_step(s)
                        norm_step(three, two)
                else:
                    if two and two.phase != s.phase:
                        norm_step(two)
                    if s.phase == GEGLU:
                        p_step(one, (0,))
                    if three:
                        stats_step(three)
                    if s.phase == GEGLU:
                        p_step(one, (1, 2, 3))
                    if one and one.phase == CROSS2:
                        ve.wait_ge(act, cnt.at("act", one, kind="qk"))
                        for t in range(T):
                            nc.vector.tensor_tensor(*masked_keys(one, 2 * t + 1), ALU.mult).then_inc(masked_dve, 1)
                    if three:
                        norm_step(three, two)
                    ve.wait_ge(full, cnt.at("full", s, kind="down"))
                    if s.phase == GEGLU:
                        ve.wait_ge(biased, cnt.at("biased", s))
                    else:
                        ve.wait_ge(summed2, cnt.at("summed2", s))
                    bank = home("down", s)
                    r = row_slice(rows if s.phase == GEGLU else rows2, s, 0, T)
                    nc.vector.tensor_tensor(r, bank[:, 0:GR], r, ALU.add).then_inc(dve, 1)

            ve.wait_ge(loaded_rows[0], 16)
            stats_step(Step(SELF, 0))
            stats_step(Step(SELF, 1))
            fold_turn(SELF)
            norm_step(Step(SELF, 0))
            fold_rest(SELF, "fa", fold_a[SELF])
            fold_rest(SELF, "fb", fold_b[SELF])
            ve.wait_ge(full, cnt.at("full", Step(SELF, 0), kind="x"))
            norm_step(Step(SELF, 1))
            fold_turn(CROSS)
            fold_rest(CROSS, "fa", fold_a[CROSS])
            fold_rest(CROSS, "fb", fold_b[CROSS])
            p_step(Step(SELF, 0), range(8))
            ve.wait_ge(loaded_rows[1], 48)
            ve.wait_ge(loaded_small, 16 * len(VECTORS))
            each_group(ve, group, looks_far=True)

        @block.gpsimd
        def _(gp):
            nc.gpsimd.memset(ident[:, :], 0.0).then_inc(made_ident, 1)
            gp.wait_ge(made_ident, 1)
            nc.gpsimd.affine_select(out=ident[:, :], in_=ident[:, :], compare_op=ALU.not_equal, fill=1.0, base=0,
                                    pattern=[[-1, 128]], channel_multiplier=1).then_inc(made_ident, 1)
            nc.gpsimd.memset(neghalf[:, :], -0.5).then_inc(made_half, 1)
            nc.gpsimd.memset(headmask[:, :], 1.0).then_inc(made_mask, 1)
            gp.wait_ge(made_mask, 1)
            nc.gpsimd.affine_select(out=headmask[:, :], in_=headmask[:, :], compare_op=ALU.is_ge, fill=0.0, base=0,
                                    pattern=[[-H1, H]], channel_multiplier=1).then_inc(made_mask, 1)
            gp.wait_ge(made_mask, 2)
            nc.gpsimd.affine_select(out=headmask[:, :], in_=headmask[:, :], compare_op=ALU.is_ge, fill=0.0, base=H1 - 1,
                                    pattern=[[H1, H]], channel_multiplier=-1).then_inc(made_mask, 1)
            for n in range(2):
                nc.gpsimd.memset(vb[n][:, :, :, :], 0.0).then_inc(made_vb, 1)
            gp.wait_ge(made_vb, 2)
            for n in range(2):
                for e in range(2):
                    one = (e + 1) * (H1 + 1) - 1
                    nc.gpsimd.memset(vb[n][64 * e:64 * e + 64, :, :, one:one + 1], 1.0).then_inc(made_vb, 1)

            def rstd_step(s):
                gp.wait_ge(epsed, cnt.at("rstd", s))
                nc.gpsimd.tensor_tensor(rstd[s.parity][:, :], veps[s.parity][:, :], neghalf[:, :], ALU.pow)\
                    .then_inc(rooted, 1)

            def bias_step(s):
                if s.phase == CROSS2:
                    return
                gp.wait_ge(normed, cnt.at("normed", s))
                buf = rows2 if s.phase == FFN else rows
                r = row_slice(buf, s, 0, T)
                r3 = r.rearrange("p (t d) -> p t d", t=T)
                b = {SELF: BO1, CROSS: BO2, GEGLU: BFF, FFN: BLAST}[s.phase]
                nc.gpsimd.tensor_tensor(r3, r3, bias[:, None, b, :].to_broadcast([ROWS, T, D]), ALU.add)\
                    .then_inc(biased, 1)
                if s.phase == FFN:
                    gp.wait_ge(biased, cnt.at("biased", s))
                    nc.gpsimd.tensor_tensor(r, r, row_slice(rows, s, 0, T), ALU.add).then_inc(summed2, 1)

            def rest_step(s):
                if s.phase == CROSS2:
                    return
                k = C if s.phase == CROSS else D
                gp.wait_ge(high, cnt.at("high", s))
                hp, rp = src[s.parity]
                nc.gpsimd.tensor_tensor(rp[0:k, :], (cT if s.phase == CROSS else xT)[s.parity][:, :],
                                        hp.bitcast(F32)[0:k, :], ALU.subtract).then_inc(rest, 1)

            def mask_step(s, group):
                gp.wait_ge(act, cnt.at("act", s, kind="qk"))
                for t in range(T):
                    if group.phase == CROSS2:
                        gp.wait_ge(scores, cnt.at("scores", group, t))
                    for b in (2 * t, 2 * t + 1) if group.phase == CROSS2 else (2 * t,):
                        last = nc.gpsimd.tensor_tensor(*masked_keys(s, b), ALU.mult)
                    last.then_inc(masked, 1)

            def group(s):
                one, two = s.ahead(1), s.ahead(2)
                three = far(s)
                if s.phase in (SELF, CROSS) or (s.phase == CROSS2 and two.phase == FFN):
                    rstd_step(two)
                if s.phase in (SELF, CROSS):
                    for t in range(T):
                        gp.wait_ge(recip, cnt.at("recip", s, t))
                        nc.gpsimd.tensor_tensor(halves(pr[t][:, :]), halves(pr[t][:, :]),
                                                rc[:, t, :, None].to_broadcast([ROWS, H, N]), ALU.mult).then_inc(probs, 1)
                    bias_step(two)
                    rest_step(two)
                    if three:
                        rstd_step(three)
                else:
                    if one and one.phase == CROSS2:
                        mask_step(one, s)
                    if three:
                        rstd_step(three)
                    if two:
                        rest_step(two)
                        bias_step(two)

            gp.wait_ge(loaded_first, 16 * len(FIRST_VECTORS))
            gp.wait_ge(made_half, 1)
            gp.wait_ge(made_mask, 3)
            gp.wait_ge(made_vb, 6)
            for g in range(2):
                rstd_step(Step(SELF, g))
            for g in range(2):
                bias_step(Step(SELF, g))
                rest_step(Step(SELF, g))
            for n, (whole, s) in enumerate(((wp, wp_s), (w1, w1_s))):
                gp.wait_ge(high_w, n + 1)
                nc.gpsimd.tensor_tensor(s[1][:, :], whole[:, :], s[0].bitcast(F32)[:, :], ALU.subtract).then_inc(rest_w, 1)
            gp.wait_ge(loaded_small, 16 * len(VECTORS))
            each_group(gp, group, looks_far=True)


_OUTS = [((B, N, D), "float32")]


def kernel(**inputs):
    import numpy as _np
    import concourse.bacc as _bacc
    from concourse import mybir as _mybir
    from concourse.bass_utils import run_bass_kernel_spmd as _run

    nc = _bacc.Bacc("TRN2", target_bir_lowering=False, num_devices=1)
    arrays, aps = {}, {}
    for name, value in inputs.items():
        a = _np.ascontiguousarray(value)
        arrays[f"in_{name}_dram"] = a
        aps[name] = nc.dram_tensor(f"in_{name}_dram", a.shape, _mybir.dt.from_np(a.dtype), kind="ExternalInput").ap()
    outs = [nc.dram_tensor(f"out_{i}_dram", shape, _mybir.dt.from_np(_np.dtype(dtype)), kind="ExternalOutput").ap()
            for i, (shape, dtype) in enumerate(_OUTS)]
    attention_blocks(nc, aps, outs[0])
    r = _run(nc, [arrays], core_ids=[0])
    return r.results[0]["out_0_dram"]
```
